# Optimizing a Trainium2 kernel written in Bass

```python
import numpy as np
import jax
import jax.numpy as jnp

def _softmax(x, axis=-1):
    return jax.nn.softmax(x, axis=axis)

def _gelu(x):
    return jax.nn.gelu(x, approximate=True)

def _silu(x):
    return jax.nn.silu(x)

def _sigmoid(x):
    return jax.nn.sigmoid(x)

def _layernorm(x, axis=-1, eps=1e-05):
    m = jnp.mean(x, axis=axis, keepdims=True)
    v = jnp.var(x, axis=axis, keepdims=True)
    return (x - m) / jnp.sqrt(v + eps)

def _scatter_add(tgt, idx, src, axis=0):
    return tgt.at[idx].add(src)

def _segment_sum(src, seg, n):
    return jax.ops.segment_sum(src, seg, n)
kernel_name = 'mk_adj_ffn_d1_adj_r2_e08ed0'

def setup_inputs(seed: int=0):
    np.random.seed(seed)
    _w = jnp.asarray

    def _rec_inputs():
        import jax
        import jax.numpy as jnp
        _gk = jax.random.key(seed)
        x = -0.0002928 + 1 * jax.random.normal(jax.random.fold_in(_gk, 1), (64, 128, 128), jnp.float32)
        _a = jax.random.bernoulli(jax.random.fold_in(_gk, 2), 0.015625, (64, 128, 128))
        _a = jnp.logical_or(_a, jnp.swapaxes(_a, -1, -2))
        _a = jnp.logical_or(_a, jnp.eye(128, dtype=bool))
        _af = _a.astype(jnp.float32)
        _af = _af * jax.random.uniform(jax.random.fold_in(_gk, 3), (64, 128, 128), jnp.float32, 0.05, 1)
        adj = _af
        return (x, adj)
    x, adj = _rec_inputs()

    def _L0_gnn_setup():
        import jax, jax.numpy as jnp
        import numpy as np
        key = jax.random.key(seed)
        k1, k2, k3, k4 = jax.random.split(key, 4)
        B, N, F_in, F_out = (8, 1024, 128, 128)
        x = jax.random.normal(k1, (B, N, F_in), dtype=jnp.float32)
        adj = jax.random.uniform(k2, (B, N, N), dtype=jnp.float32)
        stdv = 1.0 / np.sqrt(F_out)
        weight = jax.random.uniform(k3, (F_in, F_out), dtype=jnp.float32, minval=-stdv, maxval=stdv)
        bias = jax.random.uniform(k4, (F_out,), dtype=jnp.float32, minval=-stdv, maxval=stdv)
        return {'x': x, 'adj': adj, 'weight': weight, 'bias': bias}
    _L0_gnn_all = _L0_gnn_setup()
    _L0_gnn_in = {k: v for k, v in _L0_gnn_all.items() if k in ('weight', 'bias')}
    del _L0_gnn_all

    def _L0_ffn_setup():
        import jax, jax.numpy as jnp
        import numpy as np
        B, S, D, F, E, K = (8, 1024, 128, 512, 8, 2)
        key = jax.random.key(seed)
        ks = jax.random.split(key, 10)
        s = 0.02
        return {'x': jax.random.normal(ks[0], (B, S, D), dtype=jnp.float32), 'Wr': jax.random.normal(ks[1], (D, E), dtype=jnp.float32) * s, 'W1s': jax.random.normal(ks[2], (D, F), dtype=jnp.float32) * s, 'b1s': jnp.zeros((F,), dtype=jnp.float32), 'W2s': jax.random.normal(ks[3], (F, D), dtype=jnp.float32) * s, 'b2s': jnp.zeros((D,), dtype=jnp.float32), 'W1p': jax.random.normal(ks[4], (E, D, F), dtype=jnp.float32) * s, 'b1p': jnp.zeros((E, F), dtype=jnp.float32), 'W2p': jax.random.normal(ks[5], (E, F, D), dtype=jnp.float32) * s, 'b2p': jnp.zeros((E, D), dtype=jnp.float32)}
    _L0_ffn_all = _L0_ffn_setup()
    _L0_ffn_in = {k: v for k, v in _L0_ffn_all.items() if k in ('Wr', 'W1s', 'b1s', 'W2s', 'b2s', 'W1p', 'b1p', 'W2p', 'b2p')}
    del _L0_ffn_all
    return {'x': x, 'adj': adj, 'L0_gnn_weight': _L0_gnn_in['weight'], 'L0_gnn_bias': _L0_gnn_in['bias'], 'L0_ffn_Wr': _L0_ffn_in['Wr'], 'L0_ffn_W1s': _L0_ffn_in['W1s'], 'L0_ffn_b1s': _L0_ffn_in['b1s'], 'L0_ffn_W2s': _L0_ffn_in['W2s'], 'L0_ffn_b2s': _L0_ffn_in['b2s'], 'L0_ffn_W1p': _L0_ffn_in['W1p'], 'L0_ffn_b1p': _L0_ffn_in['b1p'], 'L0_ffn_W2p': _L0_ffn_in['W2p'], 'L0_ffn_b2p': _L0_ffn_in['b2p']}

def reference(x, adj, L0_gnn_weight, L0_gnn_bias, L0_ffn_Wr, L0_ffn_W1s, L0_ffn_b1s, L0_ffn_W2s, L0_ffn_b2s, L0_ffn_W1p, L0_ffn_b1p, L0_ffn_W2p, L0_ffn_b2p):
    import jax
    import jax.numpy as jnp

    def _L0_gnn_ref(x, adj, weight, bias):
        import jax, jax.numpy as jnp
        import numpy as np
        support = jnp.einsum('bni,io->bno', x, weight)
        out = jnp.einsum('bnm,bmo->bno', adj, support)
        return out + bias

    def _L0_ffn_ref(x, Wr, W1s, b1s, W2s, b2s, W1p, b1p, W2p, b2p):
        import jax, jax.numpy as jnp
        import numpy as np
        B, S, D, F, E, K = (8, 1024, 128, 512, 8, 2)
        gelu = lambda t: jax.nn.gelu(t, approximate=False)
        shared = gelu(x @ W1s + b1s) @ W2s + b2s
        rw = jax.nn.softmax(x @ Wr, axis=-1)
        topw, topi = jax.lax.top_k(rw, K)
        topw = topw / jnp.sum(topw, axis=-1, keepdims=True)
        mask = jnp.sum(jax.nn.one_hot(topi, E, dtype=topw.dtype) * topw[..., None], axis=-2)
        h = gelu(jnp.einsum('bsd,edf->bsef', x, W1p) + b1p)
        priv = jnp.einsum('bsef,efd->bsed', h, W2p) + b2p
        routed = jnp.einsum('bsed,bse->bsd', priv, mask)
        return shared + routed
    x = x + _L0_gnn_ref(_layernorm(x, axis=-1), adj, L0_gnn_weight, L0_gnn_bias)
    x = x + _L0_ffn_ref(_layernorm(x, axis=-1), L0_ffn_Wr, L0_ffn_W1s, L0_ffn_b1s, L0_ffn_W2s, L0_ffn_b2s, L0_ffn_W1p, L0_ffn_b1p, L0_ffn_W2p, L0_ffn_b2p)
    return x

_drawn_inputs = setup_inputs


def setup_inputs(seed=0):
    import zlib

    import numpy as np

    out = dict(_drawn_inputs(seed))
    spreads = {'L0_ffn_b1s': (0.0, 0.425),
     'L0_ffn_b2s': (0.0, 0.1),
     'L0_ffn_b1p': (0.0, 0.58),
     'L0_ffn_b2p': (0.0, 0.1)}
    factors = {}
    for name, (base, spread) in spreads.items():
        noise = np.random.default_rng([zlib.crc32(name.encode()), seed]).standard_normal(out[name].shape)
        drawn = base * np.exp(spread * noise) if base else spread * noise
        out[name] = jnp.asarray(drawn.astype(out[name].dtype))
    for name, factor in factors.items():
        out[name] = (out[name] * factor).astype(out[name].dtype)
    return out
```

```python
from contextlib import ExitStack

import concourse.bass as bass
from concourse import mybir

ACT = mybir.ActivationFunctionType
ALU = mybir.AluOpType
AX = mybir.AxisListType
F32 = mybir.dt.float32
F16 = mybir.dt.float16
I32 = mybir.dt.int32
U32 = mybir.dt.uint32

GRAPHS, NODES, D = 64, 128, 128
F, EXPERTS, RANKS = 512, 8, 2
TOKENS = GRAPHS * NODES
J = 4
GROUPS = GRAPHS // J
GT = J * NODES
C = F // 128
EPS = 1e-5

TILE = 256
TILES = RANKS * TOKENS // TILE + EXPERTS
REGION = TOKENS + TILE
SPARE = EXPERTS * REGION
SPARE_TILES = EXPERTS
PADS = EXPERTS + SPARE_TILES
ROW = D + 2
SHARED = EXPERTS
WSPAN = 4 * F

XS, WS, HS = 4096.0, 256.0, 64.0
BS = 1024.0


class Group:

    def __init__(self, k, u):
        self.half = k + u // 2
        self.slot = u % 2
        self.number = self.half * 2 + self.slot
        self.done = self.number + 1


class Tile:

    def __init__(self, k, v):
        self.quarter, self.slot4 = k + v // 4, v % 4
        self.half, self.slot = k * 2 + v // 2, v % 2
        self.v, self.number = v, k * 4 + v
        self.done = self.number + 1


def waiter(eng):
    def wait(sem, value):
        if not (isinstance(value, int) and value <= 0):
            eng.wait_ge(sem, value)
    return wait


def build(nc, x, adj, gw, gb, wr, w1s, b1s, w2s, b2s, w1p, b1p, w2p, b2p, out):
    routed = nc.dram_tensor("routed_rows", (SPARE + SPARE_TILES * TILE, ROW), F32, kind="Internal").ap()
    parts = nc.dram_tensor("routed_parts", (RANKS * TOKENS + PADS * TILE, D), F32, kind="Internal").ap()

    with ExitStack() as ctx:
        def sb(name, shape, dt=F32):
            return ctx.enter_context(nc.sbuf_tensor(name, shape, dt))

        def sem(name):
            return ctx.enter_context(nc.semaphore(name))

        banks = ctx.enter_context(nc.psum_tensor("banks", [128, 8, 512], F32))

        ident32, ident16 = sb("ident32", [128, 128]), sb("ident16", [128, 128], F16)
        earlier = sb("earlier", [128, 128], F16)
        ones16 = sb("ones16", [128, 128], F16)
        minus_mean = sb("minus_mean", [128, 128])
        plus_mean = sb("plus_mean", [1, 128])
        bias_gain = sb("bias_gain", [64, 128], F16)
        bias_rows = sb("bias_rows", [64, GT], F16)
        expert_no = sb("expert_no", [128, EXPERTS])
        region_start = sb("region_start", [128, J, EXPERTS])
        half_power, euler = sb("half_power", [128, J]), sb("euler", [128, J])
        bias_f = sb("bias_f", [64, GT])

        wg = sb("wg", [128, D])
        w16 = sb("w16", [128, (EXPERTS + 1) * WSPAN], F16)
        wr16 = sb("wr16", [128, 2, EXPERTS], F16)
        b2_rows, b2 = sb("b2_rows", [EXPERTS + 1, D]), sb("b2", [128, EXPERTS + 1])
        w_in = sb("w_in", [128, 2, 2, F])
        b_in = sb("b_in", [1, 2, F])
        w_shift = sb("w_shift", [128, F])
        wr_in, wr_shift = sb("wr_in", [128, EXPERTS]), sb("wr_shift", [128, EXPERTS])

        x_t = sb("x_t", [128, 2, J, D])
        adj_t = sb("adj_t", [128, 2, J, NODES])
        stats1, stats2 = sb("stats1", [128, J, 6]), sb("stats2", [128, J, 6])
        mom1, mom2 = sb("mom1", [128, J, 2]), sb("mom2", [128, J, 2])
        veps1, veps2 = sb("veps1", [128, J]), sb("veps2", [128, J])
        rstd1, rstd2 = sb("rstd1", [128, J]), sb("rstd2", [128, J])
        xn = sb("xn", [128, J, D])
        adjT = sb("adjT", [128, J, NODES])
        zT = sb("zT", [128, J, NODES])
        x2 = sb("x2", [128, GRAPHS, D])
        xs = sb("xs", [128, J, D])
        row = sb("row", [128, 2, J, RANKS, ROW])
        xT = sb("xT", [128, 2, 2, GT], F16)
        top = sb("top", [128, J, 8])
        top_at = sb("top_at", [128, J, 8], U32)
        pick_no = sb("pick_no", [128, RANKS, J])
        picks = sb("picks", [128, RANKS, J, EXPERTS], F16)
        both = sb("both", [128, J, EXPERTS], F16)
        seen = sb("seen", [128, EXPERTS], F16)
        seen_now = sb("seen_now", [128, EXPERTS])
        place = sb("place", [128, J, EXPERTS])
        place_of = sb("place_of", [128, RANKS, J, EXPERTS])
        slots = sb("slots", [128, 2, RANKS, J], I32)
        gap, gap_s, odds, den = (sb(n, [128, J]) for n in ("gap", "gap_s", "odds", "den"))
        h = sb("h", [128, 2, 512])
        h16 = sb("h16", [128, 2, 2, C, 512], F16)
        yT = sb("yT", [128, 2, 512])

        pad = sb("pad", [128, PADS, 2, ROW])
        counts = sb("counts", [1, EXPERTS])
        tiles_i, tiles_f = sb("tiles_i", [1, 2, EXPERTS], I32), sb("tiles_f", [1, EXPERTS])
        tiles_end = sb("tiles_end", [1, 4, EXPERTS])
        pad_f = sb("pad_f", [1, EXPERTS])
        pad_at = sb("pad_at", [1, EXPERTS], I32)
        tile_no = sb("tile_no", [1, TILES])
        past = sb("past", [1, TILES, EXPERTS])
        past_tiles = sb("past_tiles", [1, TILES, EXPERTS])
        tile_e, tile_before = sb("tile_e", [1, TILES]), sb("tile_before", [1, TILES])
        tile_off, tile_row_f = sb("tile_off", [1, TILES]), sb("tile_row_f", [1, TILES])
        tile_row, tile_w, tile_b = (sb(n, [1, TILES], I32) for n in ("tile_row", "tile_w", "tile_b"))
        rows = sb("rows", [128, 4, 2, ROW])
        meta = sb("meta", [128, 4, 2, 2])
        y = sb("y", [128, 2, 2, D])
        part_t = sb("part_t", [128, 2, RANKS, 8, D])
        sum_t = sb("sum_t", [128, 2, 8, D])

        row16 = row[:, :, :, :, :].bitcast(F16)
        row32 = row[:, :, :, :, :].bitcast(I32)
        rows16 = rows[:, :, :, :].bitcast(F16)
        rows32 = rows[:, :, :, :].bitcast(I32)
        meta32 = meta[:, :, :, :].bitcast(I32)
        pad32 = pad[:, :, :, :].bitcast(I32)

        bank_z = banks[:, 0, :].rearrange("p (j n) -> p j n", j=J)
        bank_g = banks[:, 1, :].rearrange("p (j n) -> p j n", j=J)
        bank_x = banks[:, 2, :].bitcast(F16).rearrange("p (a n) -> p a n", a=2)
        bank_l = banks[:, 3, :]
        logits = bank_l[:, 0:J * EXPERTS].rearrange("p (j e) -> p j e", j=J)
        before = bank_l[:, 64:64 + J * EXPERTS].rearrange("p (j e) -> p j e", j=J)
        bank_y, bank_r = banks[:, 6, :], banks[:, 7, :]

        s_const_in = sem("const_loaded")
        s_w_in = [sem(f"w_loaded{n}") for n in range(2)]
        s_x_in = [sem(f"x_loaded{n}") for n in range(2)]
        s_adj_in = [sem(f"adj_loaded{n}") for n in range(2)]
        s_scattered = [sem(f"rows_scattered{n}") for n in range(2)]
        s_spare, s_padded = sem("spare_written"), sem("padding_written")
        s_rows_in = [sem(f"rows_loaded{n}") for n in range(4)]
        s_y_out = [sem(f"y_scattered{n}") for n in range(2)]
        s_part_in = [sem(f"parts_loaded{n}") for n in range(2)]
        s_out = [sem(f"out_stored{n}") for n in range(2)]
        s_apart = sem("waits_apart")
        (s_zero, s_cpool, s_cdve, s_shift, s_w1sum, s_w1hi, s_w1lo, s_w2hi, s_w2lo, s_wr_shift, s_wrsum,
         s_wr_hi, s_wr_lo, s_gb_scaled, s_gb_hi, s_gb_lo, s_b2_turned, s_b2) = (sem(n) for n in (
             "zeroed", "pool_constants", "dve_constants", "w1_shift", "w1_sum", "w1_high", "w1_low", "w2_high",
             "w2_low", "wr_shift_s", "wr_sum", "wr_high", "wr_low", "gb_scaled", "gb_high", "gb_low", "b2_turned", "b2_ready"))
        (s_adj_turned, s_adjT, s_z, s_zT, s_g, s_x2, s_stats1, s_mom1, s_veps1, s_rstd1, s_xn, s_stats2, s_mom2,
         s_veps2, s_rstd2, s_xs, s_hi, s_lo, s_dup, s_dest, s_x_turned, s_xT, s_logits, s_top, s_top_at, s_pick_no,
         s_picks, s_both, s_before, s_seen_now, s_seen, s_place, s_place_of, s_slots, s_gap, s_gap_s, s_odds,
         s_den, s_w_first, s_w_second) = (sem(n) for n in (
             "adj_turned", "adjT_ready", "z_done", "zT_ready", "graph_done", "x2_ready", "stats1_done",
             "moments1", "var1_eps", "rstd1_ready", "xn_ready", "stats2_done", "moments2", "var2_eps",
             "rstd2_ready", "xs_ready", "x_high", "x_low", "row_copied", "dest_ready", "x_turned", "xT_ready",
             "logits_done", "top_values", "top_indices", "pick_numbers", "picks_ready", "both_ready",
             "before_done", "seen_now_s", "seen_ready", "place_ready", "place_of_ready", "slots_ready", "gap_s0",
             "gap_scaled", "odds_ready", "den_ready", "weight_first", "weight_second"))
        s_up, s_gelu, s_hhi, s_hlo = sem("up_done"), sem("gelu_done"), sem("h_high"), sem("h_low")
        s_down, s_yT, s_y_turned, s_y = sem("down_done"), sem("yT_ready"), sem("y_turned"), sem("y_ready")
        s_counts, s_table, s_chain = sem("counts_done"), sem("table_ready"), sem("table_steps")
        (t_x_turned, t_xT, t_up, t_gelu, t_hhi, t_hlo, t_down, t_yT, t_y_turned, t_y) = (sem(n) for n in (
            "tile_x_turned", "tile_xT", "tile_up", "tile_gelu", "tile_h_high", "tile_h_low", "tile_down",
            "tile_yT", "tile_y_turned", "tile_y"))
        t_meta = sem("tile_meta")
        s_part_sum, s_sum = sem("part_sum"), sem("sum_ready")

        def w16_at(base, layer, part, c):
            start = base + (2 * layer + part) * F + c * 128
            if isinstance(start, int):
                return w16[:, start:start + 128]
            return w16[:, bass.ds(start, 128)]

        def wait_apart(eng, *waits):
            waits = [(s, v) for s, v in waits if not (isinstance(v, int) and v <= 0)]
            for s, v in waits:
                eng.wait_ge(s, v)
            if not all(isinstance(v, int) for s, v in waits):
                eng.sem_inc(s_apart, 1)

        PARTS = ((0, 0), (0, 1), (1, 0))

        block = ctx.enter_context(nc.Block())

        @block.sync
        def _(sp):
            wait = waiter(sp)
            sp.dma_start(wr_in[:, :], wr).then_inc(s_const_in, 16)
            sp.dma_start(wg[:, :], gw).then_inc(s_const_in, 16)
            for j in range(J):
                for p in (0, 32):
                    sp.dma_start(bias_f[p:p + 1, j * D:(j + 1) * D],
                                 gb.rearrange("(a n) -> a n", a=1)).then_inc(s_const_in, 16)
            sp.dma_start(b2_rows[0:EXPERTS, :], b2p).then_inc(s_const_in, 16)
            sp.dma_start(b2_rows[SHARED:SHARED + 1, :], b2s.rearrange("(a d) -> a d", a=1)).then_inc(s_const_in, 16)

            for n in range(EXPERTS + 1):
                wait(s_w1sum, n - 1)
                wait(s_w2hi, n - 1)
                wait(s_w2lo, n - 1)
                first, bias, second = (w1p[n], b1p[n], w2p[n]) if n < EXPERTS else (w1s, b1s, w2s)
                sp.dma_start(b_in[:, n % 2, :], bias.rearrange("(a n) -> a n", a=1)).then_inc(s_w_in[n % 2], 16)
                sp.dma_start(w_in[:, n % 2, 0, :], first).then_inc(s_w_in[n % 2], 16)
                sp.dma_start(w_in[:, n % 2, 1, :].rearrange("p (c d) -> p c d", c=C),
                             second.rearrange("(c p) d -> p c d", p=128)).then_inc(s_w_in[n % 2], 16)

            def load(g):
                wait(s_x2, g.number - 1)
                wait(s_adj_turned, g.number - 1)
                graphs = bass.ds(g.number * J, J)
                sp.dma_start(x_t[:, g.slot, :, :], x[graphs].rearrange("b n d -> n b d")).then_inc(s_x_in[g.slot], 16)
                sp.dma_start(adj_t[:, g.slot, :, :],
                             adj[graphs].rearrange("b n d -> n b d")).then_inc(s_adj_in[g.slot], 16)

            load(Group(0, 0))
            load(Group(0, 1))
            with sp.Fori(1, GROUPS // 2) as k:
                for u in range(2):
                    load(Group(k, u))

            sp.wait_ge(s_cpool, 1)
            sp.dma_start(routed[SPARE:SPARE + SPARE_TILES * TILE, :].rearrange("(n p a) r -> p n a r", p=128, a=2),
                         pad[:, EXPERTS:PADS, :, :]).then_inc(s_spare, 16)
            for n in range(2):
                sp.wait_ge(s_scattered[n], 16 * J * RANKS * GROUPS // 2)
            sp.wait_ge(s_table, 1)
            for e in range(EXPERTS):
                at = sp.value_load(pad_at[0:1, e:e + 1], min_val=0, max_val=SPARE - TILE)
                sp.dma_start(routed[bass.ds(at, TILE), :].rearrange("(p a) r -> p a r", a=2),
                             pad[:, e, :, :]).then_inc(s_padded, 16)
            sp.wait_ge(s_padded, 16 * EXPERTS)
            sp.wait_ge(s_spare, 16)

            def load_rows(t, col):
                wait_apart(sp, (t_x_turned, t.number - 3))
                wait_apart(sp, (t_meta, t.number - 3))
                at = sp.value_load(tile_row[0:1, col], min_val=0, max_val=SPARE + (SPARE_TILES - 1) * TILE)
                sp.dma_start(rows[:, t.slot4, :, :],
                             routed[bass.ds(at, TILE), :].rearrange("(p a) r -> p a r", a=2)).then_inc(
                                 s_rows_in[t.slot4], 16)

            for n in range(4):
                load_rows(Tile(0, n), slice(n, n + 1))
            with sp.Fori(1, TILES // 4) as k:
                for v in range(4):
                    t = Tile(k, v)
                    load_rows(t, bass.ds(t.number, 1))

            for n in range(2):
                sp.wait_ge(s_y_out[n], 32 * (TILES // 2))
            part_v = parts[0:RANKS * TOKENS, :].rearrange("(r p b) d -> p r b d", r=RANKS, p=128)

            def load_parts(b):
                wait(s_part_sum, b.number - 1)
                wait(s_sum, b.number - 1)
                for r in range(RANKS):
                    sp.dma_start(part_t[:, b.slot, r, :, :],
                                 part_v[:, r, bass.ds(b.number * 8, 8), :]).then_inc(s_part_in[b.slot], 16)

            load_parts(Group(0, 0))
            load_parts(Group(0, 1))
            with sp.Fori(1, GRAPHS // 16) as k:
                for u in range(2):
                    load_parts(Group(k, u))
            for n in range(2):
                sp.wait_ge(s_out[n], 16 * (GRAPHS // 16))

        def steps(eng, step):
            for i in range(4):
                step(Group(0, i), Group(0, i - 1) if i >= 1 else None, Group(0, i - 2) if i >= 2 else None)
            with eng.Fori(2, GROUPS // 2) as k:
                for u in range(2):
                    step(Group(k, u), Group(k, u - 1), Group(k, u - 2))
            for i in (GROUPS, GROUPS + 1):
                step(None, Group(0, i - 1) if i == GROUPS else None, Group(0, i - 2))

        def tile_steps(eng, step):
            def tiles(t):
                return [Tile(0, t - n) if 0 <= t - n < TILES else None for n in range(4)]
            for t in range(4):
                step(*tiles(t))
            with eng.Fori(1, TILES // 4) as k:
                for v in range(4):
                    step(*(Tile(k, v - n) for n in range(4)))
            for t in range(TILES, TILES + 3):
                step(*tiles(t))

        @block.gpsimd
        def _(pool):
            wait = waiter(pool)
            pool.memset(ident32[:, :], 0.0)
            pool.memset(ident16[:, :], 0.0)
            pool.memset(earlier[:, :], 1.0)
            pool.memset(ones16[:, :], 1.0)
            pool.memset(minus_mean[:, :], -WS / D)
            pool.memset(plus_mean[:, :], WS / D)
            pool.memset(bias_gain[:, :], 1.0 / BS)
            pool.memset(half_power[:, :], -0.5)
            pool.memset(euler[:, :], 2.718281828459045)
            pool.memset(seen[:, :], 0.0)
            pool.memset(pad[:, :, :, :], 0.0)
            pool.memset(bias_rows[:, :], 0.0)
            pool.iota(expert_no[:, :], pattern=[[1, EXPERTS]], base=0, channel_multiplier=0,
                      allow_small_or_imprecise_dtypes=True)
            pool.iota(region_start[:, :, :], pattern=[[0, J], [REGION, EXPERTS]], base=0, channel_multiplier=0,
                      allow_small_or_imprecise_dtypes=True)
            pool.iota(tile_no[:, :], pattern=[[1, TILES]], base=0, channel_multiplier=0,
                      allow_small_or_imprecise_dtypes=True)
            for n in range(2):
                last = pool.iota(row32[:, n, :, :, D + 1], pattern=[[1, J], [TOKENS, RANKS]], base=J * n,
                                 channel_multiplier=GRAPHS)
            last.then_inc(s_zero, 1)
            pool.wait_ge(s_zero, 1)
            pool.iota(pad32[:, :, :, D + 1], pattern=[[TILE, PADS], [1, 2]], base=RANKS * TOKENS, channel_multiplier=2)
            pool.affine_select(out=ident32[:, :], in_=ident32[:, :], compare_op=ALU.not_equal, fill=1.0, base=0,
                               pattern=[[-1, 128]], channel_multiplier=1)
            pool.affine_select(out=ident16[:, :], in_=ident16[:, :], compare_op=ALU.not_equal, fill=1.0, base=0,
                               pattern=[[-1, 128]], channel_multiplier=1)
            pool.affine_select(out=earlier[:, :], in_=earlier[:, :], compare_op=ALU.is_gt, fill=0.0, base=0,
                               pattern=[[1, 128]], channel_multiplier=-1).then_inc(s_cpool, 1)

            def rstd(g, s_mom, mom, veps, s_veps, rstd_t, s_rstd, scale):
                wait_apart(pool, (s_mom, g.done))
                pool.tensor_scalar(veps[:, :], mom[:, :, 1], EPS, scale, ALU.add, ALU.mult).then_inc(s_veps, 1)
                wait(s_veps, g.done)
                pool.tensor_tensor(rstd_t[:, :], veps[:, :], half_power[:, :], ALU.pow).then_inc(s_rstd, 1)

            def weights(g):
                wait(s_top, g.done)
                pool.tensor_tensor(gap[:, :], top[:, :, 1], top[:, :, 0], ALU.subtract).then_inc(s_gap, 1)
                wait_apart(pool, (s_gap, g.done))
                pool.tensor_scalar(gap_s[:, :], gap[:, :], 1.0 / (XS * WS), None, ALU.mult).then_inc(s_gap_s, 1)
                wait(s_gap_s, g.done)
                pool.tensor_tensor(odds[:, :], euler[:, :], gap_s[:, :], ALU.pow).then_inc(s_odds, 1)
                wait_apart(pool, (s_odds, g.done))
                pool.tensor_scalar(den[:, :], odds[:, :], 1.0, None, ALU.add).then_inc(s_den, 1)

            def destinations(g):
                wait_apart(pool, (s_scattered[g.slot], g.half * (16 * J * RANKS)))
                if not (isinstance(g.number, int) and g.number < 2):
                    dest = row32[:, g.slot, :, :, D + 1]
                    pool.tensor_scalar(dest, dest, 2 * J, None, ALU.add).then_inc(s_dest, 1)

            def scatter(g, graphs):
                for j in graphs:
                    for r in range(RANKS):
                        pool.indirect_dma_start(
                            routed, bass.IndirectOffsetOnAxis(ap=slots[:, g.slot, r, j:j + 1], axis=0),
                            row[:, g.slot, j, r, :], None).then_inc(s_scattered[g.slot], 16)

            def step(g1, g2, g3):
                if g2:
                    rstd(g2, s_mom2, mom2, veps2, s_veps2, rstd2, s_rstd2, XS ** -2)
                if g1:
                    rstd(g1, s_mom1, mom1, veps1, s_veps1, rstd1, s_rstd1, 1.0)
                if g3:
                    wait_apart(pool, (s_slots, g3.done),
                               (s_lo, g3.done),
                               (s_dup, g3.done),
                               (s_w_second, g3.done),
                               (s_dest, g3.number - 1))
                    scatter(g3, range(J // 2))
                if g2:
                    destinations(g2)
                    weights(g2)
                if g3:
                    scatter(g3, range(J // 2, J))

            steps(pool, step)

            def tile_step(tx, t0, t1, t2):
                if tx:
                    wait(s_rows_in[tx.slot4], (tx.quarter + 1) * 16)
                    wait(s_y_out[tx.slot], (tx.half - 1) * 32)
                    wait_apart(pool, (t_y, tx.number - 3))
                    pool.tensor_copy(meta32[:, tx.slot4, :, :], rows32[:, tx.slot4, :, D:D + 2]).then_inc(t_meta, 1)
                if t2:
                    wait_apart(pool, (t_y, t2.done))
                    for a in range(2):
                        pool.indirect_dma_start(
                            parts, bass.IndirectOffsetOnAxis(ap=meta32[:, t2.slot4, a, 1:2], axis=0),
                            y[:, t2.slot, a, :], None).then_inc(s_y_out[t2.slot], 16)

            tile_steps(pool, tile_step)

            def add_parts(b):
                wait(s_part_in[b.slot], (b.half + 1) * 32)
                wait(s_out[b.slot], b.half * 16)
                pool.tensor_tensor(sum_t[:, b.slot, :, :], part_t[:, b.slot, 0, :, :], part_t[:, b.slot, 1, :, :],
                                   ALU.add).then_inc(s_part_sum, 1)

            add_parts(Group(0, 0))
            add_parts(Group(0, 1))
            with pool.Fori(1, GRAPHS // 16) as k:
                for u in range(2):
                    add_parts(Group(k, u))

        @block.scalar
        def _(act):
            wait = waiter(act)
            act.wait_ge(s_gb_scaled, 1)
            for p in (0, 32):
                hi = act.activation(bias_rows[p:p + 1, :], bias_f[p:p + 1, :], ACT.Copy)
            hi.then_inc(s_gb_hi, 1)
            act.wait_ge(s_wrsum, 1)
            act.activation(wr16[:, 0, :], wr_shift[:, :], ACT.Copy).then_inc(s_wr_hi, 1)
            for n in range(EXPERTS + 1):
                base = n * WSPAN
                act.wait_ge(s_w_in[n % 2], 48 * (n // 2 + 1))
                act.activation(w16[:, base + 2 * F:base + 3 * F], w_in[:, n % 2, 1, :], ACT.Copy,
                               scale=WS).then_inc(s_w2hi, 1)
                act.wait_ge(s_w1sum, n + 1)
                act.activation(w16[:, base:base + F], w_shift[:, :], ACT.Copy).then_inc(s_w1hi, 1)

            def step(g1, g2, g3):
                def gelu(c):
                    n = g3.number * C + c + 1
                    wait(s_up, n)
                    wait(s_hlo, n - 2)
                    act.activation(h[:, c % 2, :], banks[:, 4 + c % 2, :], ACT.Gelu,
                                   scale=1.0 / (XS * WS)).then_inc(s_gelu, 1)

                def high(c):
                    n = g3.number * C + c + 1
                    wait(s_gelu, n)
                    if c == 0:
                        wait(s_down, g3.number - 1)
                    act.activation(h16[:, g3.slot, 0, c, :], h[:, c % 2, :], ACT.Copy, scale=HS).then_inc(s_hhi, 1)

                if g1:
                    wait(s_adj_turned, g1.done)
                    wait(s_z, g1.number)
                    act.activation(adjT[:, :, :], bank_z, ACT.Copy).then_inc(s_adjT, 1)
                if g3:
                    gelu(0)
                    gelu(1)
                if g2:
                    wait(s_xs, g2.done)
                    wait(s_scattered[g2.slot], g2.half * (16 * J * RANKS))
                    act.activation(row16[:, g2.slot, :, 0, 0:D], xs[:, :, :], ACT.Copy, bias=XS).then_inc(s_hi, 1)
                if g3:
                    high(0)
                    high(1)
                if g1:
                    wait(s_z, g1.done)
                    wait(s_g, g1.number)
                    act.activation(zT[:, :, :], bank_z, ACT.Copy).then_inc(s_zT, 1)
                if g3:
                    gelu(2)
                if g2:
                    wait(s_x_turned, g2.done)
                    wait(s_up, (g2.number - 1) * C)
                    act.activation(xT[:, g2.slot, :, :], bank_x, ACT.Copy).then_inc(s_xT, 1)
                if g3:
                    high(2)
                    gelu(3)
                    high(3)
                if g2:
                    wait(s_lo, g2.done)
                    act.activation(row[:, g2.slot, :, 1, 0:D], row[:, g2.slot, :, 0, 0:D], ACT.Copy).then_inc(s_dup, 1)
                if g3:
                    wait(s_down, g3.done)
                    wait(s_y_turned, g3.number - 1)
                    act.activation(yT[:, g3.slot, :], bank_y, ACT.Identity, bias=b2[:, SHARED:SHARED + 1],
                                   scale=1.0 / (HS * WS)).then_inc(s_yT, 1)

            steps(act, step)

            act.wait_ge(s_table, 1)

            def tile_step(tx, t0, t1, t2):
                if t0:
                    for u in range(2):
                        n = t0.number * 2 + u + 1
                        wait(t_up, n)
                        wait(t_hlo, n - 2)
                        act.activation(h[:, u, :], banks[:, 4 + u, :], ACT.Gelu, scale=1.0 / (XS * WS)).then_inc(t_gelu, 1)
                if t1:
                    wait(t_down, t1.done)
                    wait(t_y_turned, t1.number - 1)
                    at = act.value_load(tile_b[0:1, bass.ds(t1.number, 1)], min_val=0, max_val=EXPERTS - 1)
                    act.activation(yT[:, t1.slot, 0:TILE], banks[:, 6, 0:TILE], ACT.Identity,
                                   bias=b2[:, bass.ds(at, 1)], scale=1.0 / (HS * WS)).then_inc(t_yT, 1)
                if t0:
                    for u in range(2):
                        wait(t_gelu, t0.number * 2 + u + 1)
                        wait(t_down, t0.number - 1)
                        act.activation(h16[:, t0.slot, 0, u, :], h[:, u, :], ACT.Copy, scale=HS).then_inc(t_hhi, 1)

            tile_steps(act, tile_step)

            out_v = out.rearrange("b n d -> n b d")

            def store(b):
                wait(s_sum, b.done)
                act.dma_start(out_v[:, bass.ds(b.number * 8, 8), :], sum_t[:, b.slot, :, :]).then_inc(s_out[b.slot], 16)

            store(Group(0, 0))
            store(Group(0, 1))
            with act.Fori(1, GRAPHS // 16) as k:
                for u in range(2):
                    store(Group(k, u))

        @block.tensor
        def _(pe):
            wait = waiter(pe)
            pe.wait_ge(s_cpool, 1)
            pe.wait_ge(s_const_in, 16 * (4 + 2 * J))
            pe.matmul(banks[:, 2, 0:EXPERTS], minus_mean[:, :], wr_in[:, :], start=True, stop=True).then_inc(s_wr_shift, 1)
            pe.transpose(bank_l[:, 0:EXPERTS + 1], b2_rows[:, :], ident32[0:EXPERTS + 1, 0:EXPERTS + 1]).then_inc(
                s_b2_turned, 1)
            for n in range(EXPERTS + 1):
                pe.wait_ge(s_w_in[n % 2], 48 * (n // 2 + 1))
                wait(s_w1sum, n - 1)
                pe.matmul(banks[:, n % 2, :], minus_mean[:, :], w_in[:, n % 2, 0, :], start=True, stop=False)
                pe.matmul(banks[:, n % 2, :], plus_mean[:, :], b_in[:, n % 2, :], start=False, stop=True).then_inc(s_shift, 1)
            pe.wait_ge(s_w1sum, EXPERTS + 1)
            pe.wait_ge(s_w1lo, EXPERTS + 1)
            pe.wait_ge(s_w1hi, EXPERTS + 1)
            pe.wait_ge(s_w2lo, EXPERTS + 1)
            pe.wait_ge(s_w2hi, EXPERTS + 1)
            pe.wait_ge(s_wr_lo, 1)
            pe.wait_ge(s_gb_lo, 1)
            pe.wait_ge(s_b2, 1)
            pe.wait_ge(s_wrsum, 1)

            def step(g1, g2, g3):
                def up(c):
                    n = g3.number * C + c + 1
                    wait(s_gelu, n - 2)
                    if c == 0:
                        wait(s_xT, g3.done)
                    for m, (a, b) in enumerate(PARTS):
                        mm = pe.matmul(banks[:, 4 + c % 2, :], w16_at(SHARED * WSPAN, 0, a, c), xT[:, g3.slot, b, :],
                                       start=m == 0, stop=m == 2)
                    mm.then_inc(s_up, 1)

                def down(c):
                    n = g3.number * C + c + 1
                    wait(s_hlo, n)
                    if c == 0:
                        wait(s_yT, g3.number)
                    for m, (a, b) in enumerate(PARTS):
                        mm = pe.matmul(bank_y, w16_at(SHARED * WSPAN, 1, a, c), h16[:, g3.slot, b, c, :],
                                       start=c == 0 and m == 0, stop=c == C - 1 and m == 2)
                    if c == C - 1:
                        mm.then_inc(s_down, 1)

                if g1:
                    wait(s_adj_in[g1.slot], (g1.half + 1) * 16)
                    wait(s_zT, g1.number)
                    for j in range(J):
                        mm = pe.transpose(bank_z[:, j, :], adj_t[:, g1.slot, j, :], ident32[:, :])
                    mm.then_inc(s_adj_turned, 1)
                if g3:
                    up(0)
                    up(1)
                if g1:
                    wait(s_adjT, g1.done)
                    wait(s_xn, g1.done)
                    for j in range(J):
                        mm = pe.matmul(bank_z[:, j, :], xn[:, j, :], adjT[:, j, :], start=True, stop=True)
                    mm.then_inc(s_z, 1)
                if g2:
                    wait(s_hi, g2.done)
                    wait(s_lo, g2.done)
                    wait(s_xT, g2.number)
                    for a in range(2):
                        for j in range(J):
                            mm = pe.transpose(bank_x[:, a, j * D:(j + 1) * D],
                                              row16[:, g2.slot, j, 0, a * D:(a + 1) * D], ident16[:, :])
                    mm.then_inc(s_x_turned, 1)
                if g3:
                    up(2)
                    down(0)
                if g1:
                    wait(s_zT, g1.done)
                    wait(s_x2, g1.number)
                    pe.matmul(banks[:, 1, :], bias_gain[:, :], bias_rows[:, :], start=True, stop=False,
                              skip_group_check=True)
                    for j in range(J):
                        mm = pe.matmul(bank_g[:, j, :], zT[:, j, :], wg[:, :], start=False, stop=True,
                                       skip_group_check=True)
                    mm.then_inc(s_g, 1)
                if g3:
                    up(3)
                    down(1)
                if g2:
                    wait(s_xT, g2.done)
                    wait(s_place, g2.number)
                    for j in range(J):
                        for m, (a, b) in enumerate(PARTS):
                            mm = pe.matmul(logits[:, j, :], xT[:, g2.slot, b, j * NODES:(j + 1) * NODES],
                                           wr16[:, a, :], start=m == 0, stop=m == 2)
                    mm.then_inc(s_logits, 1)
                if g3:
                    down(2)
                    down(3)
                if g2:
                    wait(s_both, g2.done)
                    wait(s_seen, g2.number)
                    pe.matmul(before, earlier[:, :], both[:, :, :], start=True, stop=False, skip_group_check=True)
                    pe.matmul(before, ones16[:, :],
                              seen[:, :].rearrange("p (a e) -> p a e", a=1).to_broadcast([128, J, EXPERTS]),
                              start=False, stop=False, skip_group_check=True)
                    for j in range(J - 1):
                        mm = pe.matmul(before[:, j + 1:J, :], ones16[:, :],
                                       both[:, j:j + 1, :].to_broadcast([128, J - 1 - j, EXPERTS]),
                                       start=False, stop=j == J - 2, skip_group_check=True)
                    mm.then_inc(s_before, 1)
                if g3:
                    wait(s_yT, g3.done)
                    wait(s_y, g3.number)
                    for j in range(J):
                        mm = pe.transpose(bank_r[:, j * D:(j + 1) * D], yT[:, g3.slot, j * D:(j + 1) * D],
                                          ident32[:, :])
                    mm.then_inc(s_y_turned, 1)

            steps(pe, step)

            pe.wait_ge(s_seen, GROUPS)
            pe.wait_ge(s_place, GROUPS)
            pe.matmul(bank_l[:, 0:EXPERTS], ones16[:, :], seen[:, :], start=True, stop=True).then_inc(s_counts, 1)

            pe.wait_ge(s_table, 1)
            pe.wait_ge(s_xT, GROUPS)
            pe.wait_ge(s_y, GROUPS)

            def turn_x(t):
                wait(s_rows_in[t.slot4], (t.quarter + 1) * 16)
                wait(t_xT, t.number)
                for a in range(2):
                    for b in range(2):
                        mm = pe.transpose(bank_x[:, b, a * 128:(a + 1) * 128],
                                          rows16[:, t.slot4, a, b * D:(b + 1) * D], ident16[:, :])
                mm.then_inc(t_x_turned, 1)

            bases = {}

            def base(t, again):
                if again or t.v not in bases:
                    bases[t.v] = pe.value_load(tile_w[0:1, bass.ds(t.number, 1)], min_val=0,
                                               max_val=(EXPERTS - 1) * WSPAN)
                return bases[t.v]

            def tile_step(tx, t0, t1, t2):
                if t0:
                    at = base(t0, True)
                    wait(t_xT, t0.done)
                    for u in range(2):
                        wait(t_gelu, t0.number * 2 + u - 1)
                        for v in range(2):
                            for m, (a, b) in enumerate(PARTS):
                                mm = pe.matmul(banks[:, 4 + u, v * TILE:(v + 1) * TILE], w16_at(at, 0, a, 2 * u + v),
                                               xT[:, t0.slot, b, 0:TILE], start=m == 0, stop=m == 2)
                        mm.then_inc(t_up, 1)
                if tx:
                    turn_x(tx)
                if t1:
                    at = base(t1, t1.v < -1 or t0 is None)
                    wait(t_yT, t1.number)
                    for u in range(2):
                        wait(t_hlo, t1.number * 2 + u + 1)
                        for v in range(2):
                            for m, (a, b) in enumerate(PARTS):
                                mm = pe.matmul(banks[:, 6, 0:TILE], w16_at(at, 1, a, 2 * u + v),
                                               h16[:, t1.slot, b, u, v * TILE:(v + 1) * TILE],
                                               start=u == 0 and v == 0 and m == 0, stop=u == 1 and v == 1 and m == 2)
                    mm.then_inc(t_down, 1)
                if t2:
                    wait(t_yT, t2.done)
                    wait(t_y, t2.number)
                    for a in range(2):
                        mm = pe.transpose(bank_r[:, a * D:(a + 1) * D], yT[:, t2.slot, a * 128:(a + 1) * 128],
                                          ident32[:, :])
                    mm.then_inc(t_y_turned, 1)

            tile_steps(pe, tile_step)

        @block.vector
        def _(dve):
            wait = waiter(dve)
            dve.wait_ge(s_const_in, 16 * (4 + 2 * J))
            dve.wait_ge(s_cpool, 1)
            for p in (0, 32):
                sc = dve.tensor_scalar(bias_f[p:p + 1, :], bias_f[p:p + 1, :], BS, None, ALU.mult)
            sc.then_inc(s_gb_scaled, 1)
            dve.wait_ge(s_gb_hi, 1)
            dve.tensor_tensor(bias_rows[32:33, :], bias_f[32:33, :], bias_rows[32:33, :], ALU.subtract).then_inc(s_gb_lo, 1)
            dve.wait_ge(s_wr_shift, 1)
            dve.scalar_tensor_tensor(out=wr_shift[:, :], in0=wr_in[:, :], scalar=WS, in1=banks[:, 2, 0:EXPERTS],
                                     op0=ALU.mult, op1=ALU.add).then_inc(s_wrsum, 1)
            dve.wait_ge(s_b2_turned, 1)
            dve.tensor_copy(b2[:, :], bank_l[:, 0:EXPERTS + 1]).then_inc(s_b2, 1)
            dve.wait_ge(s_wr_hi, 1)
            dve.tensor_tensor(wr16[:, 1, :], wr_shift[:, :], wr16[:, 0, :], ALU.subtract).then_inc(s_wr_lo, 1)
            for n in range(EXPERTS + 1):
                base = n * WSPAN
                dve.wait_ge(s_shift, n + 1)
                wait(s_w1lo, n)
                wait(s_w1hi, n)
                dve.scalar_tensor_tensor(out=w_shift[:, :], in0=w_in[:, n % 2, 0, :], scalar=WS,
                                         in1=banks[:, n % 2, :], op0=ALU.mult, op1=ALU.add).then_inc(s_w1sum, 1)
                dve.wait_ge(s_w2hi, n + 1)
                dve.scalar_tensor_tensor(out=w16[:, base + 3 * F:base + 4 * F], in0=w_in[:, n % 2, 1, :], scalar=WS,
                                         in1=w16[:, base + 2 * F:base + 3 * F], op0=ALU.mult,
                                         op1=ALU.subtract).then_inc(s_w2lo, 1)
                dve.wait_ge(s_w1hi, n + 1)
                dve.tensor_tensor(w16[:, base + F:base + 2 * F], w_shift[:, :], w16[:, base:base + F],
                                  ALU.subtract).then_inc(s_w1lo, 1)

            def graph(g):
                return x2[:, bass.ds(g.number * J, J), :]

            def moments(g, source, stats, s_stats, mom, s_mom):
                for j in range(J):
                    last = dve.bn_stats(stats[:, j, :], source(j))
                last.then_inc(s_stats, 1)
                wait_apart(dve, (s_stats, g.done))
                for j in range(J):
                    last = dve.bn_aggr(mom[:, j, :], stats[:, j, :])
                last.then_inc(s_mom, 1)

            def normalize(g, source, mom, rstd_t, to, s_to):
                for j in range(J):
                    last = dve.tensor_scalar(to[:, j, :], source(j), mom[:, j, 0:1], rstd_t[:, j:j + 1],
                                             ALU.subtract, ALU.mult)
                last.then_inc(s_to, 1)

            def step(g1, g2, g3):
                def low(c):
                    n = g3.number * C + c + 1
                    wait(s_hhi, n)
                    dve.scalar_tensor_tensor(out=h16[:, g3.slot, 1, c, :], in0=h[:, c % 2, :], scalar=HS,
                                             in1=h16[:, g3.slot, 0, c, :], op0=ALU.mult,
                                             op1=ALU.subtract).then_inc(s_hlo, 1)

                if g2:
                    wait_apart(dve, (s_x2, g2.done))
                    moments(g2, lambda j: x2[:, bass.ds(g2.number * J + j, 1), :].rearrange("p a d -> p (a d)"),
                            stats2, s_stats2, mom2, s_mom2)
                if g1:
                    wait_apart(dve, (s_x_in[g1.slot], (g1.half + 1) * 16))
                    moments(g1, lambda j: x_t[:, g1.slot, j, :], stats1, s_stats1, mom1, s_mom1)
                if g2:
                    wait(s_rstd2, g2.done)
                    wait(s_hi, g2.number)
                    wait(s_lo, g2.number)
                    normalize(g2, lambda j: x2[:, bass.ds(g2.number * J + j, 1), :].rearrange("p a d -> p (a d)"),
                              mom2, rstd2, xs, s_xs)
                if g1:
                    wait(s_rstd1, g1.done)
                    wait(s_z, g1.number)
                    normalize(g1, lambda j: x_t[:, g1.slot, j, :], mom1, rstd1, xn, s_xn)
                if g2:
                    wait(s_hi, g2.done)
                    dve.scalar_tensor_tensor(out=row16[:, g2.slot, :, 0, D:2 * D], in0=xs[:, :, :], scalar=XS,
                                             in1=row16[:, g2.slot, :, 0, 0:D], op0=ALU.add,
                                             op1=ALU.subtract).then_inc(s_lo, 1)
                if g3:
                    low(0)
                    low(1)
                if g1:
                    wait(s_g, g1.done)
                    dve.tensor_tensor(graph(g1), bank_g, x_t[:, g1.slot, :, :], ALU.add).then_inc(s_x2, 1)
                if g2:
                    wait_apart(dve, (s_logits, g2.done), (s_den, g2.number))
                    for j in range(J):
                        last = dve.max(out=top[:, j, :], in_=logits[:, j, :])
                    last.then_inc(s_top, 1)
                    wait_apart(dve, (s_top, g2.done))
                    for j in range(J):
                        last = dve.max_index(top_at[:, j, :], top[:, j, :], logits[:, j, :])
                    last.then_inc(s_top_at, 1)
                    wait(s_top_at, g2.done)
                    dve.tensor_copy(pick_no[:, :, :], top_at[:, :, 0:RANKS].rearrange("p j r -> p r j")).then_inc(
                        s_pick_no, 1)
                    wait(s_pick_no, g2.done)
                    for r in range(RANKS):
                        last = dve.tensor_tensor(
                            picks[:, r, :, :],
                            expert_no[:, :].rearrange("p (a e) -> p a e", a=1).to_broadcast([128, J, EXPERTS]),
                            pick_no[:, r, :].rearrange("p (j a) -> p j a", a=1).to_broadcast([128, J, EXPERTS]),
                            ALU.is_equal)
                    last.then_inc(s_picks, 1)
                    wait(s_picks, g2.done)
                    wait(s_before, g2.number)
                    dve.tensor_tensor(both[:, :, :], picks[:, 0, :, :], picks[:, 1, :, :], ALU.add).then_inc(s_both, 1)
                if g3:
                    low(2)
                if g2:
                    wait(s_den, g2.done)
                    wait(s_scattered[g2.slot], g2.half * (16 * J * RANKS))
                    dve.reciprocal(row[:, g2.slot, :, 0, D], den[:, :]).then_inc(s_w_first, 1)
                    wait(s_both, g2.done)
                    dve.tensor_reduce(seen_now[:, :], both[:, :, :].rearrange("p j e -> p e j"), AX.X,
                                      ALU.add).then_inc(s_seen_now, 1)
                    wait(s_w_first, g2.done)
                    dve.tensor_tensor(row[:, g2.slot, :, 1, D], odds[:, :], row[:, g2.slot, :, 0, D],
                                      ALU.mult).then_inc(s_w_second, 1)
                if g3:
                    low(3)
                if g2:
                    wait(s_before, g2.done)
                    dve.tensor_tensor(place[:, :, :], before, region_start[:, :, :], ALU.add).then_inc(s_place, 1)
                    wait(s_seen_now, g2.done)
                    dve.tensor_tensor(seen[:, :], seen[:, :], seen_now[:, :], ALU.add).then_inc(s_seen, 1)
                    wait(s_place, g2.done)
                    for r in range(RANKS):
                        last = dve.tensor_tensor(place_of[:, r, :, :], picks[:, r, :, :], place[:, :, :], ALU.mult)
                    last.then_inc(s_place_of, 1)
                    wait(s_place_of, g2.done)
                    with nc.allow_low_precision(reason="one row number of those summed is not zero"):
                        dve.tensor_reduce(slots[:, g2.slot, :, :], place_of[:, :, :, :], AX.X,
                                          ALU.add).then_inc(s_slots, 1)
                if g3:
                    wait(s_y_turned, g3.done)
                    dve.tensor_tensor(graph(g3), bank_r.rearrange("p (j d) -> p j d", j=J), graph(g3),
                                      ALU.add).then_inc(s_y, 1)

            steps(dve, step)

            links = [0]

            def link(ins):
                links[0] += 1
                ins.then_inc(s_chain, 1)
                dve.wait_ge(s_chain, links[0])

            dve.wait_ge(s_counts, 1)
            link(dve.tensor_copy(counts[:, :], bank_l[0:1, 0:EXPERTS]))
            link(dve.tensor_tensor(pad_f[:, :], counts[:, :], region_start[0:1, 0, :], ALU.add))
            link(dve.tensor_copy(pad_at[:, :], pad_f[:, :]))
            link(dve.tensor_scalar(tiles_i[:, 0, :], counts[:, :], TILE - 1.0, None, ALU.add))
            link(dve.tensor_scalar(tiles_i[:, 1, :], tiles_i[:, 0, :], TILE.bit_length() - 1, None,
                                   ALU.logical_shift_right))
            link(dve.tensor_copy(tiles_f[:, :], tiles_i[:, 1, :]))
            link(dve.tensor_copy(tiles_end[:, 0, :], tiles_f[:, :]))
            for n, s in enumerate((1, 2, 4)):
                link(dve.tensor_copy(tiles_end[:, n + 1, 0:s], tiles_end[:, n, 0:s]))
                link(dve.tensor_tensor(tiles_end[:, n + 1, s:], tiles_end[:, n, s:], tiles_end[:, n, 0:EXPERTS - s],
                                       ALU.add))
            every = [1, TILES, EXPERTS]
            over_e = lambda v: v.rearrange("p (a e) -> p a e", a=1).to_broadcast(every)
            over_t = lambda v: v.rearrange("p (t a) -> p t a", a=1).to_broadcast(every)
            link(dve.tensor_tensor(past[:, :, :], over_e(tiles_end[:, 3, :]), over_t(tile_no[:, :]), ALU.is_le))
            link(dve.tensor_reduce(tile_e[:, :], past[:, :, :], AX.X, ALU.add))
            link(dve.tensor_tensor(past_tiles[:, :, :], past[:, :, :], over_e(tiles_f[:, :]), ALU.mult))
            link(dve.tensor_reduce(tile_before[:, :], past_tiles[:, :, :], AX.X, ALU.add))
            link(dve.tensor_tensor(tile_off[:, :], tile_no[:, :], tile_before[:, :], ALU.subtract))
            link(dve.tensor_scalar(tile_off[:, :], tile_off[:, :], float(TILE), None, ALU.mult))
            link(dve.scalar_tensor_tensor(out=tile_row_f[:, :], in0=tile_e[:, :], scalar=float(REGION),
                                          in1=tile_off[:, :], op0=ALU.mult, op1=ALU.add))
            link(dve.tensor_copy(tile_row[:, :], tile_row_f[:, :]))
            link(dve.tensor_scalar(tile_b[:, :], tile_e[:, :], EXPERTS - 1.0, None, ALU.min))
            dve.tensor_scalar(tile_w[:, :], tile_b[:, :], float(WSPAN), None, ALU.mult).then_inc(s_table, 1)

            def tile_step(tx, t0, t1, t2):
                if tx:
                    wait(t_x_turned, tx.done)
                    wait(t_up, (tx.number - 1) * 2)
                    dve.tensor_copy(xT[:, tx.slot, :, 0:TILE], bank_x[:, :, 0:TILE]).then_inc(t_xT, 1)
                if t2:
                    wait(t_y_turned, t2.done)
                    wait(s_y_out[t2.slot], t2.half * 32)
                    wait(t_meta, t2.done)
                    for a in range(2):
                        last = dve.tensor_scalar(y[:, t2.slot, a, :], bank_r[:, a * D:(a + 1) * D],
                                                 meta[:, t2.slot4, a, 0:1], None, ALU.mult)
                    last.then_inc(t_y, 1)
                if t0:
                    for u in range(2):
                        wait(t_hhi, t0.number * 2 + u + 1)
                        dve.scalar_tensor_tensor(out=h16[:, t0.slot, 1, u, :], in0=h[:, u, :], scalar=HS,
                                                 in1=h16[:, t0.slot, 0, u, :], op0=ALU.mult,
                                                 op1=ALU.subtract).then_inc(t_hlo, 1)

            tile_steps(dve, tile_step)

            def add_routed(b):
                wait(s_part_sum, b.done)
                dve.tensor_tensor(sum_t[:, b.slot, :, :], x2[:, bass.ds(b.number * 8, 8), :], sum_t[:, b.slot, :, :],
                                  ALU.add).then_inc(s_sum, 1)

            add_routed(Group(0, 0))
            add_routed(Group(0, 1))
            with dve.Fori(1, GRAPHS // 16) as k:
                for u in range(2):
                    add_routed(Group(k, u))


_INS = ["x", "adj", "L0_gnn_weight", "L0_gnn_bias", "L0_ffn_Wr", "L0_ffn_W1s", "L0_ffn_b1s", "L0_ffn_W2s",
        "L0_ffn_b2s", "L0_ffn_W1p", "L0_ffn_b1p", "L0_ffn_W2p", "L0_ffn_b2p"]


def kernel(**inputs):
    import numpy as np
    import concourse.bacc as bacc
    from concourse import mybir as mb
    from concourse.bass_utils import run_bass_kernel_spmd

    nc = bacc.Bacc("TRN2", target_bir_lowering=False, num_devices=1)
    arrays, args = {}, []
    for name in _INS:
        a = np.ascontiguousarray(inputs[name])
        arrays[f"in_{name}"] = a
        args.append(nc.dram_tensor(f"in_{name}", a.shape, mb.dt.from_np(a.dtype), kind="ExternalInput").ap())
    args.append(nc.dram_tensor("out_0", (GRAPHS, NODES, D), mb.dt.from_np(np.dtype("float32")),
                               kind="ExternalOutput").ap())
    build(nc, *args)
    r = run_bass_kernel_spmd(nc, [arrays], core_ids=[0])
    return r.results[0]["out_0"]
```

```python
from contextlib import ExitStack

import concourse.bass as bass
from concourse import mybir

ACT = mybir.ActivationFunctionType
ALU = mybir.AluOpType
AX = mybir.AxisListType
F32 = mybir.dt.float32
F16 = mybir.dt.float16
I32 = mybir.dt.int32
U32 = mybir.dt.uint32

GRAPHS, NODES, D = 64, 128, 128
F, EXPERTS, RANKS = 512, 8, 2
TOKENS = GRAPHS * NODES
J = 4
GROUPS = GRAPHS // J
GT = J * NODES
C = F // 128
EPS = 1e-5

TILE = 256
TILES = RANKS * TOKENS // TILE + EXPERTS
REGION = TOKENS + TILE
SPARE = EXPERTS * REGION
SPARE_TILES = EXPERTS
PADS = EXPERTS + SPARE_TILES
ROW = D + 2
SHARED = EXPERTS
SPLIT_ORDER = (SHARED, *range(EXPERTS))
WSPAN = 4 * F

XS, WS, HS = 4096.0, 256.0, 64.0
BS = 1024.0


class Group:

    def __init__(self, k, u):
        self.half = k + u // 2
        self.slot = u % 2
        self.number = self.half * 2 + self.slot
        self.done = self.number + 1


class Tile:

    def __init__(self, k, v):
        self.quarter, self.slot4 = k + v // 4, v % 4
        self.half, self.slot = k * 2 + v // 2, v % 2
        self.v, self.number = v, k * 4 + v
        self.done = self.number + 1


def waiter(eng):
    def wait(sem, value):
        if not (isinstance(value, int) and value <= 0):
            eng.wait_ge(sem, value)
    return wait


def build(nc, x, adj, gw, gb, wr, w1s, b1s, w2s, b2s, w1p, b1p, w2p, b2p, out):
    routed = nc.dram_tensor("routed_rows", (SPARE + SPARE_TILES * TILE, ROW), F32, kind="Internal").ap()
    parts = nc.dram_tensor("routed_parts", (RANKS * TOKENS + PADS * TILE, D), F32, kind="Internal").ap()

    with ExitStack() as ctx:
        def sb(name, shape, dt=F32):
            return ctx.enter_context(nc.sbuf_tensor(name, shape, dt))

        def sem(name):
            return ctx.enter_context(nc.semaphore(name))

        banks = ctx.enter_context(nc.psum_tensor("banks", [128, 8, 512], F32))

        ident32, ident16 = sb("ident32", [128, 128]), sb("ident16", [128, 128], F16)
        earlier = sb("earlier", [128, 128], F16)
        ones16 = sb("ones16", [128, 128], F16)
        minus_mean = sb("minus_mean", [128, 128])
        plus_mean = sb("plus_mean", [1, 128])
        bias_gain = sb("bias_gain", [64, 128], F16)
        bias_rows = sb("bias_rows", [64, GT], F16)
        expert_no = sb("expert_no", [128, EXPERTS])
        region_start = sb("region_start", [128, J, EXPERTS])
        half_power = sb("half_power", [128, J])
        bias_f = sb("bias_f", [64, GT])

        wg = sb("wg", [128, D])
        w16 = sb("w16", [128, (EXPERTS + 1) * WSPAN], F16)
        wr16 = sb("wr16", [128, 2, EXPERTS], F16)
        b2_rows, b2 = sb("b2_rows", [EXPERTS + 1, D]), sb("b2", [128, EXPERTS + 1])
        w_in = sb("w_in", [128, 2, 2, F])
        b_in = sb("b_in", [1, 2, F])
        w_shift = sb("w_shift", [128, F])
        wr_in, wr_shift = sb("wr_in", [128, EXPERTS]), sb("wr_shift", [128, EXPERTS])

        x_t = sb("x_t", [128, 2, J, D])
        adj_t = sb("adj_t", [128, 2, J, NODES])
        stats1, stats2 = sb("stats1", [128, J, 6]), sb("stats2", [128, J, 6])
        mom1, mom2 = sb("mom1", [128, J, 2]), sb("mom2", [128, J, 2])
        veps1, veps2 = sb("veps1", [128, J]), sb("veps2", [128, J])
        rstd1, rstd2 = sb("rstd1", [128, J]), sb("rstd2", [128, J])
        xn = sb("xn", [128, J, D])
        adjT = sb("adjT", [128, J, NODES])
        zT = sb("zT", [128, J, NODES])
        x2 = sb("x2", [128, GRAPHS, D])
        xs = sb("xs", [128, J, D])
        x16 = sb("x16", [128, J, 2 * D], F16)
        row = sb("row", [128, 2, J, RANKS, ROW])
        xT = sb("xT", [128, 2, 2, GT], F16)
        top = sb("top", [128, J, 8])
        top_at = sb("top_at", [128, J, 8], U32)
        pick_no = sb("pick_no", [128, RANKS, J])
        picks = sb("picks", [128, RANKS, J, EXPERTS], F16)
        both = sb("both", [128, J, EXPERTS], F16)
        seen = sb("seen", [128, EXPERTS], F16)
        seen_now = sb("seen_now", [128, EXPERTS])
        place = sb("place", [128, J, EXPERTS])
        place_of = sb("place_of", [128, RANKS, J, EXPERTS])
        slots = sb("slots", [128, 2, RANKS, J], I32)
        gap, half_tanh = sb("gap", [128, J]), sb("half_tanh", [128, J])
        h = sb("h", [128, 2, 512])
        h16 = sb("h16", [128, 2, 2, C, 512], F16)
        yT = sb("yT", [128, 2, 512])

        pad = sb("pad", [128, PADS, 2, ROW])
        counts = sb("counts", [1, EXPERTS])
        tiles_i, tiles_f = sb("tiles_i", [1, 2, EXPERTS], I32), sb("tiles_f", [1, EXPERTS])
        tiles_end = sb("tiles_end", [1, 4, EXPERTS])
        pad_f = sb("pad_f", [1, EXPERTS])
        pad_at = sb("pad_at", [1, EXPERTS], I32)
        tile_no = sb("tile_no", [1, TILES])
        past = sb("past", [1, TILES, EXPERTS])
        past_tiles = sb("past_tiles", [1, TILES, EXPERTS])
        tile_e, tile_before = sb("tile_e", [1, TILES]), sb("tile_before", [1, TILES])
        tile_off, tile_row_f = sb("tile_off", [1, TILES]), sb("tile_row_f", [1, TILES])
        tile_row, tile_w, tile_b = (sb(n, [1, TILES], I32) for n in ("tile_row", "tile_w", "tile_b"))
        rows = sb("rows", [128, 4, 2, ROW])
        meta = sb("meta", [128, 4, 2, 2])
        y = sb("y", [128, 2, 2, D])
        part_t = sb("part_t", [128, 2, RANKS, 8, D])
        sum_t = sb("sum_t", [128, 2, 8, D])

        row32 = row[:, :, :, :, :].bitcast(I32)
        rows16 = rows[:, :, :, :].bitcast(F16)
        rows32 = rows[:, :, :, :].bitcast(I32)
        meta32 = meta[:, :, :, :].bitcast(I32)
        pad32 = pad[:, :, :, :].bitcast(I32)

        bank_z = banks[:, 0, :].rearrange("p (j n) -> p j n", j=J)
        bank_g = banks[:, 1, :].rearrange("p (j n) -> p j n", j=J)
        bank_x = banks[:, 2, :].bitcast(F16).rearrange("p (a n) -> p a n", a=2)
        bank_l = banks[:, 3, :]
        logits = bank_l[:, 0:J * EXPERTS].rearrange("p (j e) -> p j e", j=J)
        before = bank_l[:, 64:64 + J * EXPERTS].rearrange("p (j e) -> p j e", j=J)
        bank_y, bank_r = banks[:, 6, :], banks[:, 7, :]

        s_const_in = sem("const_loaded")
        s_w_in = [sem(f"w_loaded{n}") for n in range(2)]
        s_x_in = [sem(f"x_loaded{n}") for n in range(2)]
        s_adj_in = [sem(f"adj_loaded{n}") for n in range(2)]
        s_scattered = [sem(f"rows_scattered{n}") for n in range(2)]
        s_spare, s_padded = sem("spare_written"), sem("padding_written")
        s_rows_in = [sem(f"rows_loaded{n}") for n in range(4)]
        s_y_out = [sem(f"y_scattered{n}") for n in range(2)]
        s_part_in = [sem(f"parts_loaded{n}") for n in range(2)]
        s_out = [sem(f"out_stored{n}") for n in range(2)]
        s_apart = sem("waits_apart")
        (s_zero, s_cpool, s_cdve, s_shift, s_w1sum, s_w1hi, s_w1lo, s_w2hi, s_w2lo, s_wr_shift, s_wrsum,
         s_wr_hi, s_wr_lo, s_gb_scaled, s_gb_hi, s_gb_lo, s_b2_turned, s_b2) = (sem(n) for n in (
             "zeroed", "pool_constants", "dve_constants", "w1_shift", "w1_sum", "w1_high", "w1_low", "w2_high",
             "w2_low", "wr_shift_s", "wr_sum", "wr_high", "wr_low", "gb_scaled", "gb_high", "gb_low", "b2_turned", "b2_ready"))
        (s_adj_turned, s_adjT, s_z, s_zT, s_g, s_x2, s_stats1, s_mom1, s_xn, s_stats2, s_mom2, s_xs, s_hi, s_lo,
         s_pack, s_dest, s_x_turned, s_xT, s_logits, s_top, s_top_at, s_pick_no, s_picks, s_both, s_before,
         s_seen_now, s_seen, s_place, s_place_of, s_slots, s_gap, s_tanh, s_w_ranks) = (sem(n) for n in (
             "adj_turned", "adjT_ready", "z_done", "zT_ready", "graph_done", "x2_ready", "stats1_done", "moments1",
             "xn_ready", "stats2_done", "moments2", "xs_ready", "x_high", "x_low", "row_packed", "dest_ready",
             "x_turned", "xT_ready", "logits_done", "top_values", "top_indices", "pick_numbers", "picks_ready",
             "both_ready", "before_done", "seen_now_s", "seen_ready", "place_ready", "place_of_ready",
             "slots_ready", "gap_ready", "tanh_ready", "weights_ready"))
        s_veps1, s_veps2, s_rstd1, s_rstd2 = (sem(n) for n in ("var_eps1", "var_eps2", "rstd1_ready", "rstd2_ready"))
        s_up, s_gelu, s_hhi, s_hlo = sem("up_done"), sem("gelu_done"), sem("h_high"), sem("h_low")
        s_down, s_yT, s_y_turned, s_y = sem("down_done"), sem("yT_ready"), sem("y_turned"), sem("y_ready")
        s_counts, s_table, s_chain = sem("counts_done"), sem("table_ready"), sem("table_steps")
        (t_x_turned, t_xT, t_up, t_gelu, t_hhi, t_hlo, t_down, t_yT, t_y_turned, t_y) = (sem(n) for n in (
            "tile_x_turned", "tile_xT", "tile_up", "tile_gelu", "tile_h_high", "tile_h_low", "tile_down",
            "tile_yT", "tile_y_turned", "tile_y"))
        t_meta = sem("tile_meta")
        s_part_sum, s_sum = sem("part_sum"), sem("sum_ready")

        def w16_at(base, layer, part, c):
            start = base + (2 * layer + part) * F + c * 128
            if isinstance(start, int):
                return w16[:, start:start + 128]
            return w16[:, bass.ds(start, 128)]

        def wait_apart(eng, *waits):
            waits = [(s, v) for s, v in waits if not (isinstance(v, int) and v <= 0)]
            for s, v in waits:
                eng.wait_ge(s, v)
            if not all(isinstance(v, int) for s, v in waits):
                eng.sem_inc(s_apart, 1)

        PARTS = ((0, 0), (0, 1), (1, 0))

        block = ctx.enter_context(nc.Block())

        @block.sync
        def _(sp):
            wait = waiter(sp)
            sp.dma_start(wr_in[:, :], wr).then_inc(s_const_in, 16)
            sp.dma_start(wg[:, :], gw).then_inc(s_const_in, 16)
            for j in range(J):
                for p in (0, 32):
                    sp.dma_start(bias_f[p:p + 1, j * D:(j + 1) * D],
                                 gb.rearrange("(a n) -> a n", a=1)).then_inc(s_const_in, 16)
            sp.dma_start(b2_rows[0:EXPERTS, :], b2p).then_inc(s_const_in, 16)
            sp.dma_start(b2_rows[SHARED:SHARED + 1, :], b2s.rearrange("(a d) -> a d", a=1)).then_inc(s_const_in, 16)

            def load_weights(n):
                wait(s_w1sum, n - 1)
                wait(s_w2hi, n - 1)
                wait(s_w2lo, n - 1)
                e = SPLIT_ORDER[n]
                first, bias, second = (w1s, b1s, w2s) if e == SHARED else (w1p[e], b1p[e], w2p[e])
                sp.dma_start(b_in[:, n % 2, :], bias.rearrange("(a n) -> a n", a=1)).then_inc(s_w_in[n % 2], 16)
                sp.dma_start(w_in[:, n % 2, 0, :], first).then_inc(s_w_in[n % 2], 16)
                sp.dma_start(w_in[:, n % 2, 1, :].rearrange("p (c d) -> p c d", c=C),
                             second.rearrange("(c p) d -> p c d", p=128)).then_inc(s_w_in[n % 2], 16)

            def load(g):
                wait(s_x2, g.number - 1)
                wait(s_adj_turned, g.number - 1)
                graphs = bass.ds(g.number * J, J)
                sp.dma_start(x_t[:, g.slot, :, :], x[graphs].rearrange("b n d -> n b d")).then_inc(s_x_in[g.slot], 16)
                sp.dma_start(adj_t[:, g.slot, :, :],
                             adj[graphs].rearrange("b n d -> n b d")).then_inc(s_adj_in[g.slot], 16)

            load_weights(0)
            load(Group(0, 0))
            load_weights(1)
            load(Group(0, 1))
            for n in range(2, 6):
                load_weights(n)
            load(Group(1, 0))
            for n in range(6, EXPERTS + 1):
                load_weights(n)
            load(Group(1, 1))
            with sp.Fori(2, GROUPS // 2) as k:
                for u in range(2):
                    load(Group(k, u))

            sp.wait_ge(s_cpool, 1)
            sp.dma_start(routed[SPARE:SPARE + SPARE_TILES * TILE, :].rearrange("(n p a) r -> p n a r", p=128, a=2),
                         pad[:, EXPERTS:PADS, :, :]).then_inc(s_spare, 16)
            for n in range(2):
                sp.wait_ge(s_scattered[n], 16 * J * RANKS * GROUPS // 2)
            sp.wait_ge(s_table, 1)
            for e in range(EXPERTS):
                at = sp.value_load(pad_at[0:1, e:e + 1], min_val=0, max_val=SPARE - TILE)
                sp.dma_start(routed[bass.ds(at, TILE), :].rearrange("(p a) r -> p a r", a=2),
                             pad[:, e, :, :]).then_inc(s_padded, 16)
            sp.wait_ge(s_padded, 16 * EXPERTS)
            sp.wait_ge(s_spare, 16)

            def load_rows(t, col):
                wait_apart(sp, (t_x_turned, t.number - 3))
                wait_apart(sp, (t_meta, t.number - 3))
                at = sp.value_load(tile_row[0:1, col], min_val=0, max_val=SPARE + (SPARE_TILES - 1) * TILE)
                sp.dma_start(rows[:, t.slot4, :, :],
                             routed[bass.ds(at, TILE), :].rearrange("(p a) r -> p a r", a=2)).then_inc(
                                 s_rows_in[t.slot4], 16)

            for n in range(4):
                load_rows(Tile(0, n), slice(n, n + 1))
            with sp.Fori(1, TILES // 4) as k:
                for v in range(4):
                    t = Tile(k, v)
                    load_rows(t, bass.ds(t.number, 1))

            for n in range(2):
                sp.wait_ge(s_y_out[n], 32 * (TILES // 2))
            part_v = parts[0:RANKS * TOKENS, :].rearrange("(r p b) d -> p r b d", r=RANKS, p=128)

            def load_parts(b):
                wait(s_part_sum, b.number - 1)
                wait(s_sum, b.number - 1)
                for r in range(RANKS):
                    sp.dma_start(part_t[:, b.slot, r, :, :],
                                 part_v[:, r, bass.ds(b.number * 8, 8), :]).then_inc(s_part_in[b.slot], 16)

            load_parts(Group(0, 0))
            load_parts(Group(0, 1))
            with sp.Fori(1, GRAPHS // 16) as k:
                for u in range(2):
                    load_parts(Group(k, u))
            for n in range(2):
                sp.wait_ge(s_out[n], 16 * (GRAPHS // 16))

        def steps(eng, step, depth):
            peeled = (depth + 3) // 2 * 2
            def lagged(i):
                return [Group(0, i - lag) if 0 <= i - lag < GROUPS else None for lag in range(depth + 1)]
            for i in range(peeled):
                step(i, lagged(i))
            with eng.Fori(peeled // 2, GROUPS // 2) as k:
                for u in range(2):
                    step(None, [Group(k, u - lag) for lag in range(depth + 1)])
            for i in range(GROUPS, GROUPS + depth):
                step(i, lagged(i))

        def tile_steps(eng, step):
            def tiles(t):
                return [Tile(0, t - n) if 0 <= t - n < TILES else None for n in range(4)]
            for t in range(4):
                step(*tiles(t))
            with eng.Fori(1, TILES // 4) as k:
                for v in range(4):
                    step(*(Tile(k, v - n) for n in range(4)))
            for t in range(TILES, TILES + 3):
                step(*tiles(t))

        @block.gpsimd
        def _(pool):
            wait = waiter(pool)
            pool.memset(ident32[:, :], 0.0)
            pool.memset(ident16[:, :], 0.0)
            pool.memset(earlier[:, :], 1.0)
            pool.memset(ones16[:, :], 1.0)
            pool.memset(minus_mean[:, :], -WS / D)
            pool.memset(plus_mean[:, :], WS / D)
            pool.memset(bias_gain[:, :], 1.0 / BS)
            pool.memset(half_power[:, :], -0.5)
            pool.memset(seen[:, :], 0.0)
            pool.memset(pad[:, :, :, :], 0.0)
            pool.memset(bias_rows[:, :], 0.0)
            pool.iota(expert_no[:, :], pattern=[[1, EXPERTS]], base=0, channel_multiplier=0,
                      allow_small_or_imprecise_dtypes=True)
            pool.iota(region_start[:, :, :], pattern=[[0, J], [REGION, EXPERTS]], base=0, channel_multiplier=0,
                      allow_small_or_imprecise_dtypes=True)
            pool.iota(tile_no[:, :], pattern=[[1, TILES]], base=0, channel_multiplier=0,
                      allow_small_or_imprecise_dtypes=True)
            for n in range(2):
                last = pool.iota(row32[:, n, :, :, D + 1], pattern=[[1, J], [TOKENS, RANKS]], base=J * n,
                                 channel_multiplier=GRAPHS)
            last.then_inc(s_zero, 1)
            pool.wait_ge(s_zero, 1)
            pool.iota(pad32[:, :, :, D + 1], pattern=[[TILE, PADS], [1, 2]], base=RANKS * TOKENS, channel_multiplier=2)
            pool.affine_select(out=ident32[:, :], in_=ident32[:, :], compare_op=ALU.not_equal, fill=1.0, base=0,
                               pattern=[[-1, 128]], channel_multiplier=1)
            pool.affine_select(out=ident16[:, :], in_=ident16[:, :], compare_op=ALU.not_equal, fill=1.0, base=0,
                               pattern=[[-1, 128]], channel_multiplier=1)
            pool.affine_select(out=earlier[:, :], in_=earlier[:, :], compare_op=ALU.is_gt, fill=0.0, base=0,
                               pattern=[[1, 128]], channel_multiplier=-1).then_inc(s_cpool, 1)

            def rstd_of_x(g):
                if not g:
                    return
                wait(s_veps1, g.done)
                wait(s_xn, g.number)
                pool.tensor_tensor(rstd1[:, :], veps1[:, :], half_power[:, :], ALU.pow).then_inc(s_rstd1, 1)

            def rstd_of_x2(g):
                if not g:
                    return
                wait(s_veps2, g.done)
                wait(s_xs, g.number)
                pool.tensor_tensor(rstd2[:, :], veps2[:, :], half_power[:, :], ALU.pow).then_inc(s_rstd2, 1)

            def destinations(g):
                if not g or (isinstance(g.number, int) and g.number < 2):
                    return
                wait_apart(pool, (s_scattered[g.slot], g.half * (16 * J * RANKS)))
                dest = row32[:, g.slot, :, :, D + 1]
                pool.tensor_scalar(dest, dest, 2 * J, None, ALU.add).then_inc(s_dest, 1)

            def scatter(g, j):
                if not g:
                    return
                if j == 0:
                    wait_apart(pool, (s_slots, g.done), (s_pack, g.done), (s_w_ranks, g.done), (s_dest, g.number - 1))
                for r in range(RANKS):
                    pool.indirect_dma_start(
                        routed, bass.IndirectOffsetOnAxis(ap=slots[:, g.slot, r, j:j + 1], axis=0),
                        row[:, g.slot, j, r, :], None).then_inc(s_scattered[g.slot], 16)

            def step(i, g):
                rstd_of_x(g[0])
                scatter(g[3], 0)
                rstd_of_x2(g[1])
                scatter(g[3], 1)
                scatter(g[3], 2)
                scatter(g[3], 3)
                destinations(g[1])

            steps(pool, step, 3)

            def tile_step(tx, t0, t1, t2):
                if tx:
                    wait(s_rows_in[tx.slot4], (tx.quarter + 1) * 16)
                    wait(s_y_out[tx.slot], (tx.half - 1) * 32)
                    wait_apart(pool, (t_y, tx.number - 3))
                    pool.tensor_copy(meta32[:, tx.slot4, :, :], rows32[:, tx.slot4, :, D:D + 2]).then_inc(t_meta, 1)
                if t2:
                    wait_apart(pool, (t_y, t2.done))
                    for a in range(2):
                        pool.indirect_dma_start(
                            parts, bass.IndirectOffsetOnAxis(ap=meta32[:, t2.slot4, a, 1:2], axis=0),
                            y[:, t2.slot, a, :], None).then_inc(s_y_out[t2.slot], 16)

            tile_steps(pool, tile_step)

            def add_parts(b):
                wait(s_part_in[b.slot], (b.half + 1) * 32)
                wait(s_out[b.slot], b.half * 16)
                pool.tensor_tensor(sum_t[:, b.slot, :, :], part_t[:, b.slot, 0, :, :], part_t[:, b.slot, 1, :, :],
                                   ALU.add).then_inc(s_part_sum, 1)

            add_parts(Group(0, 0))
            add_parts(Group(0, 1))
            with pool.Fori(1, GRAPHS // 16) as k:
                for u in range(2):
                    add_parts(Group(k, u))

        @block.scalar
        def _(act):
            wait = waiter(act)
            act.wait_ge(s_gb_scaled, 1)
            for p in (0, 32):
                hi = act.activation(bias_rows[p:p + 1, :], bias_f[p:p + 1, :], ACT.Copy)
            hi.then_inc(s_gb_hi, 1)
            act.wait_ge(s_wrsum, 1)
            act.activation(wr16[:, 0, :], wr_shift[:, :], ACT.Copy).then_inc(s_wr_hi, 1)
            def split_weights(n):
                base = SPLIT_ORDER[n] * WSPAN
                act.wait_ge(s_w_in[n % 2], 48 * (n // 2 + 1))
                act.activation(w16[:, base + 2 * F:base + 3 * F], w_in[:, n % 2, 1, :], ACT.Copy,
                               scale=WS).then_inc(s_w2hi, 1)
                act.wait_ge(s_w1sum, n + 1)
                act.activation(w16[:, base:base + F], w_shift[:, :], ACT.Copy).then_inc(s_w1hi, 1)

            split_weights(0)

            def gelu(g, u):
                if not g:
                    return
                m = g.number * C + u + 1
                wait(s_up, m)
                wait(s_hlo, m - 2)
                act.activation(h[:, u % 2, :], banks[:, 4 + u % 2, :], ACT.Gelu,
                               scale=1.0 / (XS * WS)).then_inc(s_gelu, 1)

            def high(g, u):
                if not g:
                    return
                wait(s_gelu, g.number * C + u + 1)
                if u == 0:
                    wait(s_down, g.number - 1)
                act.activation(h16[:, g.slot, 0, u, :], h[:, u % 2, :], ACT.Copy, scale=HS).then_inc(s_hhi, 1)

            def x_high(g):
                if not g:
                    return
                wait(s_xs, g.done)
                wait(s_x_turned, g.number)
                wait(s_pack, g.number)
                act.activation(x16[:, :, 0:D], xs[:, :, :], ACT.Copy, bias=XS).then_inc(s_hi, 1)

            def copy_zT(g):
                if not g:
                    return
                wait(s_z, g.done)
                wait(s_g, g.number)
                act.activation(zT[:, :, :], bank_z, ACT.Copy).then_inc(s_zT, 1)

            def copy_adjT(g):
                if not g:
                    return
                wait(s_adj_turned, g.done)
                wait(s_z, g.number)
                act.activation(adjT[:, :, :], bank_z, ACT.Copy).then_inc(s_adjT, 1)

            def copy_xT(g):
                if not g:
                    return
                wait(s_x_turned, g.done)
                wait(s_up, (g.number - 1) * C)
                wait(s_logits, g.number - 1)
                act.activation(xT[:, g.slot, :, :], bank_x, ACT.Copy).then_inc(s_xT, 1)

            def gap_tanh(g):
                if not g:
                    return
                wait(s_gap, g.done)
                wait(s_w_ranks, g.number)
                act.activation(half_tanh[:, :], gap[:, :], ACT.Tanh, scale=0.5 / (XS * WS)).then_inc(s_tanh, 1)

            def pack_rows(g):
                if not g:
                    return
                wait(s_lo, g.done)
                wait(s_scattered[g.slot], g.half * (16 * J * RANKS))
                act.activation(row[:, g.slot, :, :, 0:D],
                               x16[:, :, :].bitcast(F32).rearrange("p j (r d) -> p j r d", r=1).to_broadcast(
                                   [128, J, RANKS, D]), ACT.Copy).then_inc(s_pack, 1)

            def bias_yT(g):
                if not g:
                    return
                wait(s_down, g.done)
                wait(s_y_turned, g.number - 1)
                act.activation(yT[:, g.slot, :], bank_y, ACT.Identity, bias=b2[:, SHARED:SHARED + 1],
                               scale=1.0 / (HS * WS)).then_inc(s_yT, 1)

            def step(i, g):
                if i == 0:
                    split_weights(1)
                if i == 1:
                    split_weights(4)
                copy_adjT(g[0])
                pack_rows(g[2])
                if i == 0:
                    split_weights(2)
                if i == 0:
                    split_weights(3)
                if i == 1:
                    split_weights(5)
                if i == 1:
                    split_weights(6)
                if i == 2:
                    split_weights(8)
                copy_zT(g[0])
                gelu(g[3], 3)
                high(g[3], 2)
                x_high(g[1])
                gap_tanh(g[2])
                high(g[3], 3)
                gelu(g[2], 0)
                bias_yT(g[4])
                if i == 1:
                    split_weights(7)
                copy_xT(g[1])
                high(g[2], 0)
                gelu(g[2], 1)
                high(g[2], 1)
                gelu(g[2], 2)

            steps(act, step, 4)

            act.wait_ge(s_table, 1)

            def tile_step(tx, t0, t1, t2):
                if t0:
                    for u in range(2):
                        n = t0.number * 2 + u + 1
                        wait(t_up, n)
                        wait(t_hlo, n - 2)
                        act.activation(h[:, u, :], banks[:, 4 + u, :], ACT.Gelu, scale=1.0 / (XS * WS)).then_inc(t_gelu, 1)
                if t1:
                    wait(t_down, t1.done)
                    wait(t_y_turned, t1.number - 1)
                    at = act.value_load(tile_b[0:1, bass.ds(t1.number, 1)], min_val=0, max_val=EXPERTS - 1)
                    act.activation(yT[:, t1.slot, 0:TILE], banks[:, 6, 0:TILE], ACT.Identity,
                                   bias=b2[:, bass.ds(at, 1)], scale=1.0 / (HS * WS)).then_inc(t_yT, 1)
                if t0:
                    for u in range(2):
                        wait(t_gelu, t0.number * 2 + u + 1)
                        wait(t_down, t0.number - 1)
                        act.activation(h16[:, t0.slot, 0, u, :], h[:, u, :], ACT.Copy, scale=HS).then_inc(t_hhi, 1)

            tile_steps(act, tile_step)

            out_v = out.rearrange("b n d -> n b d")

            def store(b):
                wait(s_sum, b.done)
                act.dma_start(out_v[:, bass.ds(b.number * 8, 8), :], sum_t[:, b.slot, :, :]).then_inc(s_out[b.slot], 16)

            store(Group(0, 0))
            store(Group(0, 1))
            with act.Fori(1, GRAPHS // 16) as k:
                for u in range(2):
                    store(Group(k, u))

        @block.tensor
        def _(pe):
            wait = waiter(pe)
            pe.wait_ge(s_cpool, 1)
            pe.wait_ge(s_const_in, 16 * (4 + 2 * J))
            pe.matmul(banks[:, 2, 0:EXPERTS], minus_mean[:, :], wr_in[:, :], start=True, stop=True).then_inc(s_wr_shift, 1)
            pe.transpose(bank_l[:, 0:EXPERTS + 1], b2_rows[:, :], ident32[0:EXPERTS + 1, 0:EXPERTS + 1]).then_inc(
                s_b2_turned, 1)
            def shift_weights(n):
                pe.wait_ge(s_w_in[n % 2], 48 * (n // 2 + 1))
                wait(s_w1sum, n - 1)
                bank = banks[:, 6 + n % 2, :]
                pe.matmul(bank, minus_mean[:, :], w_in[:, n % 2, 0, :], start=True, stop=False)
                pe.matmul(bank, plus_mean[:, :], b_in[:, n % 2, :], start=False, stop=True).then_inc(s_shift, 1)

            shift_weights(0)
            pe.wait_ge(s_w1sum, 1)
            pe.wait_ge(s_w1lo, 1)
            pe.wait_ge(s_w1hi, 1)
            pe.wait_ge(s_w2lo, 1)
            pe.wait_ge(s_w2hi, 1)
            pe.wait_ge(s_wr_lo, 1)
            pe.wait_ge(s_gb_lo, 1)
            pe.wait_ge(s_b2, 1)
            pe.wait_ge(s_wrsum, 1)

            def up(g, u):
                if not g:
                    return
                wait(s_gelu, g.number * C + u - 1)
                if u == 0:
                    wait(s_xT, g.done)
                for m, (a, b) in enumerate(PARTS):
                    mm = pe.matmul(banks[:, 4 + u % 2, :], w16_at(SHARED * WSPAN, 0, a, u), xT[:, g.slot, b, :],
                                   start=m == 0, stop=m == 2)
                mm.then_inc(s_up, 1)

            def down(g, u):
                if not g:
                    return
                if u == 0 and isinstance(g.number, int) and g.number == 0:
                    pe.wait_ge(s_w1sum, EXPERTS + 1)
                wait(s_hlo, g.number * C + u + 1)
                if u == 0:
                    wait(s_yT, g.number)
                for m, (a, b) in enumerate(PARTS):
                    mm = pe.matmul(bank_y, w16_at(SHARED * WSPAN, 1, a, u), h16[:, g.slot, b, u, :],
                                   start=u == 0 and m == 0, stop=u == C - 1 and m == 2)
                if u == C - 1:
                    mm.then_inc(s_down, 1)

            def turn_y(g):
                if not g:
                    return
                wait(s_yT, g.done)
                wait(s_y, g.number)
                for j in range(J):
                    mm = pe.transpose(bank_r[:, j * D:(j + 1) * D], yT[:, g.slot, j * D:(j + 1) * D], ident32[:, :])
                mm.then_inc(s_y_turned, 1)

            def turn_adj(g):
                if not g:
                    return
                wait(s_adj_in[g.slot], (g.half + 1) * 16)
                wait(s_zT, g.number)
                for j in range(J):
                    mm = pe.transpose(bank_z[:, j, :], adj_t[:, g.slot, j, :], ident32[:, :])
                mm.then_inc(s_adj_turned, 1)

            def aggregate(g):
                if not g:
                    return
                wait(s_adjT, g.done)
                wait(s_xn, g.done)
                for j in range(J):
                    mm = pe.matmul(bank_z[:, j, :], xn[:, j, :], adjT[:, j, :], start=True, stop=True)
                mm.then_inc(s_z, 1)

            def graph_product(g):
                if not g:
                    return
                wait(s_zT, g.done)
                wait(s_x2, g.number)
                pe.matmul(banks[:, 1, :], bias_gain[:, :], bias_rows[:, :], start=True, stop=False,
                          skip_group_check=True)
                for j in range(J):
                    mm = pe.matmul(bank_g[:, j, :], zT[:, j, :], wg[:, :], start=False, stop=True,
                                   skip_group_check=True)
                mm.then_inc(s_g, 1)

            def turn_x_group(g):
                if not g:
                    return
                wait(s_hi, g.done)
                wait(s_lo, g.done)
                wait(s_xT, g.number)
                for a in range(2):
                    for j in range(J):
                        mm = pe.transpose(bank_x[:, a, j * D:(j + 1) * D], x16[:, j, a * D:(a + 1) * D],
                                          ident16[:, :])
                mm.then_inc(s_x_turned, 1)

            def router_logits(g):
                if not g:
                    return
                wait(s_xT, g.done)
                wait(s_top_at, g.number)
                wait(s_place, g.number)
                for j in range(J):
                    for m, (a, b) in enumerate(PARTS):
                        mm = pe.matmul(logits[:, j, :], xT[:, g.slot, b, j * NODES:(j + 1) * NODES],
                                       wr16[:, a, :], start=m == 0, stop=m == 2)
                mm.then_inc(s_logits, 1)

            def count_before(g):
                if not g:
                    return
                wait(s_both, g.done)
                wait(s_seen, g.number)
                wait(s_top_at, g.done)
                pe.matmul(before, earlier[:, :], both[:, :, :], start=True, stop=False, skip_group_check=True)
                pe.matmul(before, ones16[:, :],
                          seen[:, :].rearrange("p (a e) -> p a e", a=1).to_broadcast([128, J, EXPERTS]),
                          start=False, stop=False, skip_group_check=True)
                for j in range(J - 1):
                    mm = pe.matmul(before[:, j + 1:J, :], ones16[:, :],
                                   both[:, j:j + 1, :].to_broadcast([128, J - 1 - j, EXPERTS]),
                                   start=False, stop=j == J - 2, skip_group_check=True)
                mm.then_inc(s_before, 1)

            def step(i, g):
                if i == 2:
                    shift_weights(6)
                graph_product(g[1])
                count_before(g[3])
                down(g[5], 3)
                turn_x_group(g[2])
                if i == 0:
                    shift_weights(1)
                if i == 1:
                    shift_weights(4)
                turn_adj(g[0])
                up(g[3], 2)
                if i == 2:
                    shift_weights(7)
                router_logits(g[2])
                down(g[4], 0)
                up(g[3], 3)
                down(g[4], 1)
                up(g[2], 0)
                if i == 0:
                    shift_weights(2)
                if i == 0:
                    shift_weights(3)
                if i == 1:
                    shift_weights(5)
                if i == 2:
                    shift_weights(8)
                aggregate(g[0])
                turn_y(g[5])
                down(g[4], 2)
                up(g[2], 1)

            steps(pe, step, 5)

            pe.wait_ge(s_seen, GROUPS)
            pe.wait_ge(s_place, GROUPS)
            pe.matmul(bank_l[:, 0:EXPERTS], ones16[:, :], seen[:, :], start=True, stop=True).then_inc(s_counts, 1)

            pe.wait_ge(s_table, 1)
            pe.wait_ge(s_xT, GROUPS)
            pe.wait_ge(s_y, GROUPS)
            pe.wait_ge(s_w1lo, EXPERTS + 1)
            pe.wait_ge(s_w1hi, EXPERTS + 1)
            pe.wait_ge(s_w2lo, EXPERTS + 1)
            pe.wait_ge(s_w2hi, EXPERTS + 1)

            def turn_x(t):
                wait(s_rows_in[t.slot4], (t.quarter + 1) * 16)
                wait(t_xT, t.number)
                for a in range(2):
                    for b in range(2):
                        mm = pe.transpose(bank_x[:, b, a * 128:(a + 1) * 128],
                                          rows16[:, t.slot4, a, b * D:(b + 1) * D], ident16[:, :])
                mm.then_inc(t_x_turned, 1)

            bases = {}

            def base(t, again):
                if again or t.v not in bases:
                    bases[t.v] = pe.value_load(tile_w[0:1, bass.ds(t.number, 1)], min_val=0,
                                               max_val=(EXPERTS - 1) * WSPAN)
                return bases[t.v]

            def tile_step(tx, t0, t1, t2):
                if t0:
                    at = base(t0, True)
                    wait(t_xT, t0.done)
                    for u in range(2):
                        wait(t_gelu, t0.number * 2 + u - 1)
                        for v in range(2):
                            for m, (a, b) in enumerate(PARTS):
                                mm = pe.matmul(banks[:, 4 + u, v * TILE:(v + 1) * TILE], w16_at(at, 0, a, 2 * u + v),
                                               xT[:, t0.slot, b, 0:TILE], start=m == 0, stop=m == 2)
                        mm.then_inc(t_up, 1)
                if tx:
                    turn_x(tx)
                if t1:
                    at = base(t1, t1.v < -1 or t0 is None)
                    wait(t_yT, t1.number)
                    for u in range(2):
                        wait(t_hlo, t1.number * 2 + u + 1)
                        for v in range(2):
                            for m, (a, b) in enumerate(PARTS):
                                mm = pe.matmul(banks[:, 6, 0:TILE], w16_at(at, 1, a, 2 * u + v),
                                               h16[:, t1.slot, b, u, v * TILE:(v + 1) * TILE],
                                               start=u == 0 and v == 0 and m == 0, stop=u == 1 and v == 1 and m == 2)
                    mm.then_inc(t_down, 1)
                if t2:
                    wait(t_yT, t2.done)
                    wait(t_y, t2.number)
                    for a in range(2):
                        mm = pe.transpose(bank_r[:, a * D:(a + 1) * D], yT[:, t2.slot, a * 128:(a + 1) * 128],
                                          ident32[:, :])
                    mm.then_inc(t_y_turned, 1)

            tile_steps(pe, tile_step)

        @block.vector
        def _(dve):
            wait = waiter(dve)
            dve.wait_ge(s_const_in, 16 * (4 + 2 * J))
            dve.wait_ge(s_cpool, 1)
            for p in (0, 32):
                sc = dve.tensor_scalar(bias_f[p:p + 1, :], bias_f[p:p + 1, :], BS, None, ALU.mult)
            sc.then_inc(s_gb_scaled, 1)
            dve.wait_ge(s_gb_hi, 1)
            dve.tensor_tensor(bias_rows[32:33, :], bias_f[32:33, :], bias_rows[32:33, :], ALU.subtract).then_inc(s_gb_lo, 1)
            dve.wait_ge(s_wr_shift, 1)
            dve.scalar_tensor_tensor(out=wr_shift[:, :], in0=wr_in[:, :], scalar=WS, in1=banks[:, 2, 0:EXPERTS],
                                     op0=ALU.mult, op1=ALU.add).then_inc(s_wrsum, 1)
            dve.wait_ge(s_b2_turned, 1)
            dve.tensor_copy(b2[:, :], bank_l[:, 0:EXPERTS + 1]).then_inc(s_b2, 1)
            dve.wait_ge(s_wr_hi, 1)
            dve.tensor_tensor(wr16[:, 1, :], wr_shift[:, :], wr16[:, 0, :], ALU.subtract).then_inc(s_wr_lo, 1)
            def split_weights(n):
                base = SPLIT_ORDER[n] * WSPAN
                dve.wait_ge(s_shift, n + 1)
                wait(s_w1lo, n)
                wait(s_w1hi, n)
                dve.scalar_tensor_tensor(out=w_shift[:, :], in0=w_in[:, n % 2, 0, :], scalar=WS,
                                         in1=banks[:, 6 + n % 2, :], op0=ALU.mult, op1=ALU.add).then_inc(s_w1sum, 1)
                dve.wait_ge(s_w2hi, n + 1)
                dve.scalar_tensor_tensor(out=w16[:, base + 3 * F:base + 4 * F], in0=w_in[:, n % 2, 1, :], scalar=WS,
                                         in1=w16[:, base + 2 * F:base + 3 * F], op0=ALU.mult,
                                         op1=ALU.subtract).then_inc(s_w2lo, 1)
                dve.wait_ge(s_w1hi, n + 1)
                dve.tensor_tensor(w16[:, base + F:base + 2 * F], w_shift[:, :], w16[:, base:base + F],
                                  ALU.subtract).then_inc(s_w1lo, 1)

            split_weights(0)

            def x2_of(g):
                return x2[:, bass.ds(g.number * J, J), :]

            def x2_graph(g, j):
                return x2[:, bass.ds(g.number * J + j, 1), :].rearrange("p a d -> p (a d)")

            def stats_of_x(g):
                if not g:
                    return
                wait_apart(dve, (s_x_in[g.slot], (g.half + 1) * 16))
                for j in range(J):
                    last = dve.bn_stats(stats1[:, j, :], x_t[:, g.slot, j, :])
                last.then_inc(s_stats1, 1)

            def moments_of_x(g):
                if not g:
                    return
                wait_apart(dve, (s_stats1, g.done))
                for j in range(J):
                    last = dve.bn_aggr(mom1[:, j, :], stats1[:, j, :])
                last.then_inc(s_mom1, 1)

            def variance_of_x(g):
                if not g:
                    return
                wait(s_mom1, g.done)
                wait(s_rstd1, g.number)
                dve.tensor_scalar(veps1[:, :], mom1[:, :, 1], EPS, None, ALU.add).then_inc(s_veps1, 1)

            def normalize1(g):
                if not g:
                    return
                wait(s_rstd1, g.done)
                wait(s_z, g.number)
                for j in range(J):
                    last = dve.tensor_scalar(xn[:, j, :], x_t[:, g.slot, j, :], mom1[:, j, 0:1], rstd1[:, j:j + 1],
                                             ALU.subtract, ALU.mult)
                last.then_inc(s_xn, 1)

            def add_graph(g):
                if not g:
                    return
                wait(s_g, g.done)
                dve.tensor_tensor(x2_of(g), bank_g, x_t[:, g.slot, :, :], ALU.add).then_inc(s_x2, 1)

            def stats_of_x2(g):
                if not g:
                    return
                wait_apart(dve, (s_x2, g.done))
                for j in range(J):
                    last = dve.bn_stats(stats2[:, j, :], x2_graph(g, j))
                last.then_inc(s_stats2, 1)

            def moments_of_x2(g):
                if not g:
                    return
                wait_apart(dve, (s_stats2, g.done))
                for j in range(J):
                    last = dve.bn_aggr(mom2[:, j, :], stats2[:, j, :])
                last.then_inc(s_mom2, 1)

            def variance_of_x2(g):
                if not g:
                    return
                wait(s_mom2, g.done)
                wait(s_rstd2, g.number)
                dve.tensor_scalar(veps2[:, :], mom2[:, :, 1], EPS, XS ** -2, ALU.add, ALU.mult).then_inc(s_veps2, 1)

            def normalize2(g):
                if not g:
                    return
                wait(s_rstd2, g.done)
                wait(s_hi, g.number)
                wait(s_lo, g.number)
                for j in range(J):
                    last = dve.tensor_scalar(xs[:, j, :], x2_graph(g, j), mom2[:, j, 0:1], rstd2[:, j:j + 1],
                                             ALU.subtract, ALU.mult)
                last.then_inc(s_xs, 1)

            def x_low(g):
                if not g:
                    return
                wait(s_hi, g.done)
                dve.scalar_tensor_tensor(out=x16[:, :, D:2 * D], in0=xs[:, :, :], scalar=XS,
                                         in1=x16[:, :, 0:D], op0=ALU.add, op1=ALU.subtract).then_inc(s_lo, 1)

            def top_values(g):
                if not g:
                    return
                wait_apart(dve, (s_logits, g.done))
                for j in range(J):
                    last = dve.max(out=top[:, j, :], in_=logits[:, j, :])
                last.then_inc(s_top, 1)

            def top_indices(g):
                if not g:
                    return
                wait_apart(dve, (s_top, g.done))
                for j in range(J):
                    last = dve.max_index(top_at[:, j, :], top[:, j, :], logits[:, j, :])
                last.then_inc(s_top_at, 1)

            def logit_gap(g):
                if not g:
                    return
                wait(s_top, g.done)
                wait(s_tanh, g.number)
                dve.tensor_tensor(gap[:, :], top[:, :, 0], top[:, :, 1], ALU.subtract).then_inc(s_gap, 1)

            def router_weights(g):
                if not g:
                    return
                wait(s_tanh, g.done)
                wait(s_scattered[g.slot], g.half * (16 * J * RANKS))
                for r in range(RANKS):
                    last = dve.tensor_scalar(row[:, g.slot, :, r, D], half_tanh[:, :], 0.5 - r, 0.5,
                                             ALU.mult, ALU.add)
                last.then_inc(s_w_ranks, 1)

            def pick_numbers(g):
                if not g:
                    return
                wait(s_top_at, g.done)
                dve.tensor_copy(pick_no[:, :, :], top_at[:, :, 0:RANKS].rearrange("p j r -> p r j")).then_inc(
                    s_pick_no, 1)

            def one_hots(g):
                if not g:
                    return
                wait(s_pick_no, g.done)
                for r in range(RANKS):
                    last = dve.tensor_tensor(
                        picks[:, r, :, :],
                        expert_no[:, :].rearrange("p (a e) -> p a e", a=1).to_broadcast([128, J, EXPERTS]),
                        pick_no[:, r, :].rearrange("p (j a) -> p j a", a=1).to_broadcast([128, J, EXPERTS]),
                        ALU.is_equal)
                last.then_inc(s_picks, 1)

            def both_picks(g):
                if not g:
                    return
                wait(s_picks, g.done)
                wait(s_before, g.number)
                dve.tensor_tensor(both[:, :, :], picks[:, 0, :, :], picks[:, 1, :, :], ALU.add).then_inc(s_both, 1)

            def count_picks(g):
                if not g:
                    return
                wait(s_both, g.done)
                dve.tensor_reduce(seen_now[:, :], both[:, :, :].rearrange("p j e -> p e j"), AX.X,
                                  ALU.add).then_inc(s_seen_now, 1)

            def add_to_seen(g):
                if not g:
                    return
                wait(s_seen_now, g.done)
                wait(s_before, g.done)
                dve.tensor_tensor(seen[:, :], seen[:, :], seen_now[:, :], ALU.add).then_inc(s_seen, 1)

            def places(g):
                if not g:
                    return
                wait(s_before, g.done)
                dve.tensor_tensor(place[:, :, :], before, region_start[:, :, :], ALU.add).then_inc(s_place, 1)

            def places_of_picks(g):
                if not g:
                    return
                wait(s_place, g.done)
                for r in range(RANKS):
                    last = dve.tensor_tensor(place_of[:, r, :, :], picks[:, r, :, :], place[:, :, :], ALU.mult)
                last.then_inc(s_place_of, 1)

            def row_numbers(g):
                if not g:
                    return
                wait(s_place_of, g.done)
                wait(s_scattered[g.slot], g.half * (16 * J * RANKS))
                with nc.allow_low_precision(reason="one row number of those summed is not zero"):
                    dve.tensor_reduce(slots[:, g.slot, :, :], place_of[:, :, :, :], AX.X,
                                      ALU.add).then_inc(s_slots, 1)

            def low(g, u):
                if not g:
                    return
                wait(s_hhi, g.number * C + u + 1)
                dve.scalar_tensor_tensor(out=h16[:, g.slot, 1, u, :], in0=h[:, u % 2, :], scalar=HS,
                                         in1=h16[:, g.slot, 0, u, :], op0=ALU.mult,
                                         op1=ALU.subtract).then_inc(s_hlo, 1)

            def add_shared(g):
                if not g:
                    return
                wait(s_y_turned, g.done)
                dve.tensor_tensor(x2_of(g), bank_r.rearrange("p (j d) -> p j d", j=J), x2_of(g),
                                  ALU.add).then_inc(s_y, 1)

            def step(i, g):
                if i == 2:
                    split_weights(5)
                variance_of_x2(g[2])
                count_picks(g[4])
                normalize1(g[1])
                if i == 3:
                    split_weights(8)
                top_indices(g[3])
                low(g[4], 1)
                logit_gap(g[3])
                pick_numbers(g[3])
                add_to_seen(g[4])
                normalize2(g[2])
                one_hots(g[3])
                if i == 0:
                    split_weights(1)
                if i == 1:
                    split_weights(3)
                if i == 2:
                    split_weights(6)
                stats_of_x(g[0])
                add_shared(g[6])
                both_picks(g[3])
                low(g[4], 2)
                x_low(g[2])
                low(g[4], 3)
                moments_of_x(g[0])
                places(g[3])
                router_weights(g[3])
                if i == 0:
                    split_weights(2)
                variance_of_x(g[0])
                places_of_picks(g[3])
                if i == 1:
                    split_weights(4)
                add_graph(g[1])
                row_numbers(g[3])
                if i == 2:
                    split_weights(7)
                stats_of_x2(g[1])
                low(g[3], 0)
                moments_of_x2(g[1])
                top_values(g[2])

            steps(dve, step, 6)

            links = [0]

            def link(ins):
                links[0] += 1
                ins.then_inc(s_chain, 1)
                dve.wait_ge(s_chain, links[0])

            dve.wait_ge(s_counts, 1)
            link(dve.tensor_copy(counts[:, :], bank_l[0:1, 0:EXPERTS]))
            link(dve.tensor_tensor(pad_f[:, :], counts[:, :], region_start[0:1, 0, :], ALU.add))
            link(dve.tensor_copy(pad_at[:, :], pad_f[:, :]))
            link(dve.tensor_scalar(tiles_i[:, 0, :], counts[:, :], TILE - 1.0, None, ALU.add))
            link(dve.tensor_scalar(tiles_i[:, 1, :], tiles_i[:, 0, :], TILE.bit_length() - 1, None,
                                   ALU.logical_shift_right))
            link(dve.tensor_copy(tiles_f[:, :], tiles_i[:, 1, :]))
            link(dve.tensor_copy(tiles_end[:, 0, :], tiles_f[:, :]))
            for n, s in enumerate((1, 2, 4)):
                link(dve.tensor_copy(tiles_end[:, n + 1, 0:s], tiles_end[:, n, 0:s]))
                link(dve.tensor_tensor(tiles_end[:, n + 1, s:], tiles_end[:, n, s:], tiles_end[:, n, 0:EXPERTS - s],
                                       ALU.add))
            every = [1, TILES, EXPERTS]
            over_e = lambda v: v.rearrange("p (a e) -> p a e", a=1).to_broadcast(every)
            over_t = lambda v: v.rearrange("p (t a) -> p t a", a=1).to_broadcast(every)
            link(dve.tensor_tensor(past[:, :, :], over_e(tiles_end[:, 3, :]), over_t(tile_no[:, :]), ALU.is_le))
            link(dve.tensor_reduce(tile_e[:, :], past[:, :, :], AX.X, ALU.add))
            link(dve.tensor_tensor(past_tiles[:, :, :], past[:, :, :], over_e(tiles_f[:, :]), ALU.mult))
            link(dve.tensor_reduce(tile_before[:, :], past_tiles[:, :, :], AX.X, ALU.add))
            link(dve.tensor_tensor(tile_off[:, :], tile_no[:, :], tile_before[:, :], ALU.subtract))
            link(dve.tensor_scalar(tile_off[:, :], tile_off[:, :], float(TILE), None, ALU.mult))
            link(dve.scalar_tensor_tensor(out=tile_row_f[:, :], in0=tile_e[:, :], scalar=float(REGION),
                                          in1=tile_off[:, :], op0=ALU.mult, op1=ALU.add))
            link(dve.tensor_copy(tile_row[:, :], tile_row_f[:, :]))
            link(dve.tensor_scalar(tile_b[:, :], tile_e[:, :], EXPERTS - 1.0, None, ALU.min))
            dve.tensor_scalar(tile_w[:, :], tile_b[:, :], float(WSPAN), None, ALU.mult).then_inc(s_table, 1)

            def tile_step(tx, t0, t1, t2):
                if tx:
                    wait(t_x_turned, tx.done)
                    wait(t_up, (tx.number - 1) * 2)
                    dve.tensor_copy(xT[:, tx.slot, :, 0:TILE], bank_x[:, :, 0:TILE]).then_inc(t_xT, 1)
                if t2:
                    wait(t_y_turned, t2.done)
                    wait(s_y_out[t2.slot], t2.half * 32)
                    wait(t_meta, t2.done)
                    for a in range(2):
                        last = dve.tensor_scalar(y[:, t2.slot, a, :], bank_r[:, a * D:(a + 1) * D],
                                                 meta[:, t2.slot4, a, 0:1], None, ALU.mult)
                    last.then_inc(t_y, 1)
                if t0:
                    for u in range(2):
                        wait(t_hhi, t0.number * 2 + u + 1)
                        dve.scalar_tensor_tensor(out=h16[:, t0.slot, 1, u, :], in0=h[:, u, :], scalar=HS,
                                                 in1=h16[:, t0.slot, 0, u, :], op0=ALU.mult,
                                                 op1=ALU.subtract).then_inc(t_hlo, 1)

            tile_steps(dve, tile_step)

            def add_routed(b):
                wait(s_part_sum, b.done)
                dve.tensor_tensor(sum_t[:, b.slot, :, :], x2[:, bass.ds(b.number * 8, 8), :], sum_t[:, b.slot, :, :],
                                  ALU.add).then_inc(s_sum, 1)

            add_routed(Group(0, 0))
            add_routed(Group(0, 1))
            with dve.Fori(1, GRAPHS // 16) as k:
                for u in range(2):
                    add_routed(Group(k, u))


_INS = ["x", "adj", "L0_gnn_weight", "L0_gnn_bias", "L0_ffn_Wr", "L0_ffn_W1s", "L0_ffn_b1s", "L0_ffn_W2s",
        "L0_ffn_b2s", "L0_ffn_W1p", "L0_ffn_b1p", "L0_ffn_W2p", "L0_ffn_b2p"]


def kernel(**inputs):
    import numpy as np
    import concourse.bacc as bacc
    from concourse import mybir as mb
    from concourse.bass_utils import run_bass_kernel_spmd

    nc = bacc.Bacc("TRN2", target_bir_lowering=False, num_devices=1)
    arrays, args = {}, []
    for name in _INS:
        a = np.ascontiguousarray(inputs[name])
        arrays[f"in_{name}"] = a
        args.append(nc.dram_tensor(f"in_{name}", a.shape, mb.dt.from_np(a.dtype), kind="ExternalInput").ap())
    args.append(nc.dram_tensor("out_0", (GRAPHS, NODES, D), mb.dt.from_np(np.dtype("float32")),
                               kind="ExternalOutput").ap())
    build(nc, *args)
    r = run_bass_kernel_spmd(nc, [arrays], core_ids=[0])
    return r.results[0]["out_0"]
```

```python
from contextlib import ExitStack

import concourse.bass as bass
from concourse import mybir

ACT = mybir.ActivationFunctionType
ALU = mybir.AluOpType
AX = mybir.AxisListType
F32 = mybir.dt.float32
F16 = mybir.dt.float16
I32 = mybir.dt.int32
U32 = mybir.dt.uint32

GRAPHS, NODES, D = 64, 128, 128
F, EXPERTS, RANKS = 512, 8, 2
TOKENS = GRAPHS * NODES
J = 4
GROUPS = GRAPHS // J
GT = J * NODES
C = F // 128
EPS = 1e-5

TILE = 256
TILES = RANKS * TOKENS // TILE + EXPERTS - 1
REGION = TOKENS + TILE
SPARE = EXPERTS * REGION
SPARE_TILES = EXPERTS - 1
PADS = EXPERTS + SPARE_TILES
ROW = D + 2
SHARED = EXPERTS
SPLIT_ORDER = (SHARED, *range(EXPERTS))
WSPAN = 4 * F + 2 * D

XS, WS, HS = 4096.0, 256.0, 64.0
BS = 1024.0

BLOCK = 4
BLOCKS, SLOTS = GRAPHS // BLOCK, 4


class Block:

    def __init__(self, k, v):
        self.number, self.slot, self.uses = k * SLOTS + v, v, k
        self.done = self.number + 1
        self.graphs = bass.ds(self.number * BLOCK, BLOCK)


class Group:

    def __init__(self, k, u):
        self.half = k + u // 2
        self.slot = u % 2
        self.number = self.half * 2 + self.slot
        self.done = self.number + 1


class Tile:

    def __init__(self, k, v):
        self.quarter, self.slot4 = k + v // 4, v % 4
        self.half, self.slot = k * 2 + v // 2, v % 2
        self.v, self.number = v, k * 4 + v
        self.done = self.number + 1


def waiter(eng):
    def wait(sem, value):
        if not (isinstance(value, int) and value <= 0):
            eng.wait_ge(sem, value)
    return wait


def build(nc, x, adj, gw, gb, wr, w1s, b1s, w2s, b2s, w1p, b1p, w2p, b2p, out):
    routed = nc.dram_tensor("routed_rows", (SPARE + SPARE_TILES * TILE, ROW), F32, kind="Internal").ap()
    parts = nc.dram_tensor("routed_parts", (RANKS * TOKENS + PADS * TILE, D), F32, kind="Internal").ap()

    with ExitStack() as ctx:
        def sb(name, shape, dt=F32):
            return ctx.enter_context(nc.sbuf_tensor(name, shape, dt))

        def sem(name):
            return ctx.enter_context(nc.semaphore(name))

        banks = ctx.enter_context(nc.psum_tensor("banks", [128, 8, 512], F32))

        ident32, ident16 = sb("ident32", [128, 128]), sb("ident16", [128, 128], F16)
        earlier = sb("earlier", [128, 128], F16)
        ones16 = sb("ones16", [128, 128], F16)
        minus_mean = sb("minus_mean", [128, 128])
        plus_mean = sb("plus_mean", [1, 128])
        bias_gain = sb("bias_gain", [64, 128], F16)
        out_gain = sb("out_gain", [64, 128], F16)
        bias_rows = sb("bias_rows", [64, D], F16)
        expert_no = sb("expert_no", [128, EXPERTS])
        region_start = sb("region_start", [128, J, EXPERTS])
        half_power = sb("half_power", [128, J])
        bias_f = sb("bias_f", [64, D])

        wg = sb("wg", [128, D])
        w16 = sb("w16", [128, (EXPERTS + 1) * WSPAN - 2 * D], F16)
        wr16 = sb("wr16", [128, 2, EXPERTS], F16)
        b2_f, b2_16 = sb("b2_f", [64, D]), sb("b2_16", [64, D], F16)
        w_in = sb("w_in", [128, 2, 2, F])
        b_in = sb("b_in", [1, 2, F])
        w_shift = sb("w_shift", [128, F])
        wr_in, wr_shift = sb("wr_in", [128, EXPERTS]), sb("wr_shift", [128, EXPERTS])

        x_t = sb("x_t", [128, 2, J, D])
        adj_t = sb("adj_t", [128, 2, J, NODES])
        stats1, stats2 = sb("stats1", [128, J, 6]), sb("stats2", [128, J, 6])
        mom1, mom2 = sb("mom1", [128, J, 2]), sb("mom2", [128, J, 2])
        veps1, veps2 = sb("veps1", [128, J]), sb("veps2", [128, J])
        rstd1, rstd2 = sb("rstd1", [128, J]), sb("rstd2", [128, J])
        xn, xn_bias = sb("xn", [128, J, D]), sb("xn_bias", [128, J])
        adjT = sb("adjT", [128, J, NODES])
        zT = sb("zT", [128, J, NODES])
        x2 = sb("x2", [128, GRAPHS, D])
        xs = sb("xs", [128, J, D])
        x16 = sb("x16", [128, J, 2 * D], F16)
        row = sb("row", [128, 2, J, RANKS, ROW])
        xT = sb("xT", [128, 2, 2, GT], F16)
        top = sb("top", [128, J, 8])
        top_at = sb("top_at", [128, J, 8], U32)
        pick_no = sb("pick_no", [128, RANKS, J])
        picks = sb("picks", [128, RANKS, J, EXPERTS], F16)
        both = sb("both", [128, J, EXPERTS], F16)
        seen = sb("seen", [128, EXPERTS], F16)
        seen_now = sb("seen_now", [128, EXPERTS])
        place = sb("place", [128, J, EXPERTS])
        place_of = sb("place_of", [128, RANKS, J, EXPERTS])
        slots = sb("slots", [128, 2, RANKS, J], I32)
        gap, half_tanh = sb("gap", [128, J]), sb("half_tanh", [128, J])
        h = sb("h", [128, 2, 512])
        h16 = sb("h16", [128, 2, 2, C, 512], F16)

        pad = sb("pad", [128, PADS, 2, ROW])
        counts = sb("counts", [1, EXPERTS])
        tiles_i = sb("tiles_i", [1, 2, EXPERTS], I32)
        tiles_end, region_step = sb("tiles_end", [1, 4, EXPERTS]), sb("region_step", [1, EXPERTS])
        pad_at = sb("pad_at", [1, EXPERTS], I32)
        tile_no = sb("tile_no", [1, TILES])
        past, past_steps = sb("past", [1, TILES, EXPERTS]), sb("past_steps", [1, TILES, EXPERTS])
        tile_e, row_steps = sb("tile_e", [1, TILES]), sb("row_steps", [1, TILES])
        tile_row = sb("tile_row", [1, TILES], I32)
        tile_w, tile_word = sb("tile_w", [1, TILES], I32), sb("tile_word", [1, TILES], I32)
        rows = sb("rows", [128, 4, 2, ROW])
        w2_t = sb("w2_t", [128, 4, 2 * F + 2 * D], F16)
        y_b = sb("y_b", [128, 2, 2, D])
        meta = sb("meta", [128, 4, 2, 2])
        y = sb("y", [128, 2, 2, D])
        part_t = sb("part_t", [128, SLOTS, RANKS, BLOCK, D])

        row32 = row[:, :, :, :, :].bitcast(I32)
        rows16 = rows[:, :, :, :].bitcast(F16)
        rows32 = rows[:, :, :, :].bitcast(I32)
        meta32 = meta[:, :, :, :].bitcast(I32)
        pad32 = pad[:, :, :, :].bitcast(I32)

        bank_z = banks[:, 0, :].rearrange("p (j n) -> p j n", j=J)
        bank_g = banks[:, 1, :].rearrange("p (j n) -> p j n", j=J)
        bank_x = banks[:, 2, :].bitcast(F16).rearrange("p (a n) -> p a n", a=2)
        bank_l = banks[:, 3, :]
        logits = bank_l[:, 0:J * EXPERTS].rearrange("p (j e) -> p j e", j=J)
        before = bank_l[:, 64:64 + J * EXPERTS].rearrange("p (j e) -> p j e", j=J)
        b2_private = w16[:, 0:EXPERTS * WSPAN].bitcast(F32).rearrange("p (e s) -> p e s", e=EXPERTS)[:, :, 2 * F:WSPAN // 2]
        w2_t32 = w2_t[:, :, :].bitcast(F32)
        w_words, w2_words = w16[:, :].bitcast(I32), w2_t[:, :, :].bitcast(I32)

        def bank_y(slot):
            return banks[:, 6 + slot, :]

        s_const_in, s_b2_in, s_b2_private_in = sem("const_loaded"), sem("b2_loaded"), sem("private_b2_loaded")
        s_w_in = [sem(f"w_loaded{n}") for n in range(2)]
        s_x_in = [sem(f"x_loaded{n}") for n in range(2)]
        s_adj_in = [sem(f"adj_loaded{n}") for n in range(2)]
        s_scattered = [sem(f"rows_scattered{n}") for n in range(2)]
        s_spare, s_padded = sem("spare_written"), sem("padding_written")
        s_rows_in = [sem(f"rows_loaded{n}") for n in range(4)]
        s_w2_in = [sem(f"w2_copied{n}") for n in range(4)]
        s_y_out = [sem(f"y_scattered{n}") for n in range(2)]
        s_part_in = [sem(f"parts_loaded{n}") for n in range(SLOTS)]
        s_out = sem("out_stored")
        s_apart = sem("waits_apart")
        (s_zero, s_rows_zero, s_cpool, s_pad, s_shift, s_w1sum, s_w1hi, s_w1lo, s_w2hi, s_w2lo, s_wr_shift, s_wrsum,
         s_wr_hi, s_wr_lo, s_gb_scaled, s_gb_hi, s_gb_lo, s_b2_scaled, s_b2_hi, s_b2_lo) = (sem(n) for n in (
             "zeroed", "bias_rows_zeroed", "pool_constants", "padding_ready", "w1_shift", "w1_sum", "w1_high", "w1_low", "w2_high",
             "w2_low", "wr_shift_s", "wr_sum", "wr_high", "wr_low", "gb_scaled", "gb_high", "gb_low",
             "b2_scaled", "b2_high", "b2_low"))
        (s_adj_turned, s_adjT, s_z, s_zT, s_g, s_x2, s_stats1, s_mom1, s_xn_bias, s_xn, s_stats2, s_mom2, s_xs, s_hi, s_lo,
         s_pack, s_dest, s_x_turned, s_xT, s_logits, s_top, s_top_at, s_pick_no, s_picks, s_both, s_before,
         s_seen_now, s_seen, s_place, s_place_of, s_slots, s_gap, s_tanh, s_w_ranks) = (sem(n) for n in (
             "adj_turned", "adjT_ready", "z_done", "zT_ready", "graph_done", "x2_ready", "stats1_done", "moments1",
             "xn_bias_ready", "xn_ready", "stats2_done", "moments2", "xs_ready", "x_high", "x_low", "row_packed", "dest_ready",
             "x_turned", "xT_ready", "logits_done", "top_values", "top_indices", "pick_numbers", "picks_ready",
             "both_ready", "before_done", "seen_now_s", "seen_ready", "place_ready", "place_of_ready",
             "slots_ready", "gap_ready", "tanh_ready", "weights_ready"))
        s_veps1, s_veps2, s_rstd1, s_rstd2 = (sem(n) for n in ("var_eps1", "var_eps2", "rstd1_ready", "rstd2_ready"))
        s_up, s_gelu, s_hhi, s_hlo = sem("up_done"), sem("gelu_done"), sem("h_high"), sem("h_low")
        s_down, s_y = sem("down_done"), sem("y_ready")
        s_counts, s_table, s_chain = sem("counts_done"), sem("table_ready"), sem("table_steps")
        s_pad_at = sem("padding_rows_ready")
        (t_x_turned, t_xT, t_up, t_gelu, t_hhi, t_hlo, t_down, t_y_b, t_y) = (sem(n) for n in (
            "tile_x_turned", "tile_xT", "tile_up", "tile_gelu", "tile_h_high", "tile_h_low", "tile_down",
            "tile_y_with_bias", "tile_y"))
        t_meta = sem("tile_meta")
        s_part_sum, s_sum = sem("part_sum"), sem("sum_ready")

        def w16_at(base, layer, part, c):
            start = base + (2 * layer + part) * F + c * 128
            if isinstance(start, int):
                return w16[:, start:start + 128]
            return w16[:, bass.ds(start, 128)]

        def wait_apart(eng, *waits):
            waits = [(s, v) for s, v in waits if not (isinstance(v, int) and v <= 0)]
            for s, v in waits:
                eng.wait_ge(s, v)
            if not all(isinstance(v, int) for s, v in waits):
                eng.sem_inc(s_apart, 1)

        PARTS = ((0, 0), (0, 1), (1, 0))

        def blocks(eng, step):
            for v in range(SLOTS):
                step(Block(0, v))
            with eng.Fori(1, BLOCKS // SLOTS) as k:
                for v in range(SLOTS):
                    step(Block(k, v))

        block = ctx.enter_context(nc.Block())

        @block.sync
        def _(sp):
            wait = waiter(sp)

            def load_constants():
                sp.dma_start(wr_in[:, :], wr).then_inc(s_const_in, 16)
                sp.dma_start(wg[:, :], gw).then_inc(s_const_in, 16)
                sp.wait_ge(s_rows_zero, 1)
                for p in (0, 32):
                    sp.dma_start(bias_f[p:p + 1, :], gb.rearrange("(a n) -> a n", a=1)).then_inc(s_const_in, 16)

            def load_b2():
                for p in (0, 32):
                    sp.dma_start(b2_f[p:p + 1, :], b2s.rearrange("(a d) -> a d", a=1)).then_inc(s_b2_in, 16)
                sp.dma_start(b2_private, b2p.rearrange("(a e) d -> a e d", a=1).to_broadcast([128, EXPERTS, D])).then_inc(
                    s_b2_private_in, 16)

            def load_weights(n):
                wait(s_w1sum, n - 1)
                wait(s_w2hi, n - 1)
                wait(s_w2lo, n - 1)
                e = SPLIT_ORDER[n]
                first, bias, second = (w1s, b1s, w2s) if e == SHARED else (w1p[e], b1p[e], w2p[e])
                sp.dma_start(b_in[:, n % 2, :], bias.rearrange("(a n) -> a n", a=1)).then_inc(s_w_in[n % 2], 16)
                sp.dma_start(w_in[:, n % 2, 0, :], first).then_inc(s_w_in[n % 2], 16)
                sp.dma_start(w_in[:, n % 2, 1, :].rearrange("p (c d) -> p c d", c=C),
                             second.rearrange("(c p) d -> p c d", p=128)).then_inc(s_w_in[n % 2], 16)

            def load_x(g):
                wait(s_x2, g.number - 1)
                sp.dma_start(x_t[:, g.slot, :, :],
                             x[bass.ds(g.number * J, J)].rearrange("b n d -> n b d")).then_inc(s_x_in[g.slot], 16)

            def load_adj(g):
                wait(s_adj_turned, g.number - 1)
                sp.dma_start(adj_t[:, g.slot, :, :],
                             adj[bass.ds(g.number * J, J)].rearrange("b n d -> n b d")).then_inc(s_adj_in[g.slot], 16)

            load_x(Group(0, 0))
            load_x(Group(0, 1))
            load_constants()
            load_weights(0)
            load_adj(Group(0, 0))
            load_adj(Group(0, 1))
            load_weights(1)
            load_b2()
            load_adj(Group(0, 2))
            load_weights(2)
            load_weights(3)
            load_adj(Group(0, 3))
            load_x(Group(0, 2))
            load_weights(4)
            load_adj(Group(0, 4))
            load_x(Group(0, 3))
            load_weights(5)
            load_adj(Group(0, 5))
            load_x(Group(0, 4))
            load_weights(6)
            load_weights(7)
            load_x(Group(0, 5))
            load_weights(8)
            with sp.Fori(3, GROUPS // 2) as k:
                for u in range(2):
                    load_x(Group(k, u))
                    load_adj(Group(k, u))

            sp.wait_ge(s_pad, 1)
            sp.dma_start(routed[SPARE:SPARE + SPARE_TILES * TILE, :].rearrange("(n p a) r -> p n a r", p=128, a=2),
                         pad[:, EXPERTS:PADS, :, :]).then_inc(s_spare, 16)
            sp.wait_ge(s_pad_at, 1)
            for e in range(EXPERTS):
                at = sp.value_load(pad_at[0:1, e:e + 1], min_val=0, max_val=SPARE - TILE)
                sp.dma_start(routed[bass.ds(at, TILE), :].rearrange("(p a) r -> p a r", a=2),
                             pad[:, e, :, :]).then_inc(s_padded, 16)
            sp.wait_ge(s_table, 1)

            def load_rows(t, col):
                wait_apart(sp, (t_x_turned, t.number - 3))
                wait_apart(sp, (t_meta, t.number - 3))
                at = sp.value_load(tile_row[0:1, col], min_val=0, max_val=SPARE + (SPARE_TILES - 1) * TILE)
                sp.dma_start(rows[:, t.slot4, :, :],
                             routed[bass.ds(at, TILE), :].rearrange("(p a) r -> p a r", a=2)).then_inc(
                                 s_rows_in[t.slot4], 16)

            def load_w2(t, col):
                at = sp.value_load(tile_word[0:1, col], min_val=0, max_val=(EXPERTS - 1) * WSPAN // 2)
                wait_apart(sp, (t_y_b, t.number - 3))
                sp.dma_start(w2_words[:, t.slot4, :], w_words[:, bass.ds(at + F, F + D)]).then_inc(s_w2_in[t.slot4], 16)

            sp.wait_ge(s_b2_private_in, 16)
            for n in range(2):
                load_w2(Tile(0, n), slice(n, n + 1))
            for n in range(2):
                sp.wait_ge(s_scattered[n], 16 * J * RANKS * GROUPS // 2)
            sp.wait_ge(s_padded, 16 * EXPERTS)
            sp.wait_ge(s_spare, 16)
            for n in range(4):
                load_rows(Tile(0, n), slice(n, n + 1))
            for n in range(2, 4):
                load_w2(Tile(0, n), slice(n, n + 1))
            with sp.Fori(1, TILES // 4) as k:
                for v in range(4):
                    t = Tile(k, v)
                    load_rows(t, bass.ds(t.number, 1))
                    load_w2(t, bass.ds(t.number, 1))
            for n in range(TILES // 4 * 4, TILES):
                load_rows(Tile(0, n), slice(n, n + 1))
                load_w2(Tile(0, n), slice(n, n + 1))

            for n in range(2):
                sp.wait_ge(s_y_out[n], 32 * ((TILES + 1 - n) // 2))
            part_v = parts[0:RANKS * TOKENS, :].rearrange("(r p b) d -> p r b d", r=RANKS, p=128)

            def load_parts(b):
                wait(s_sum, b.number - SLOTS + 1)
                for r in range(RANKS):
                    sp.dma_start(part_t[:, b.slot, r, :, :],
                                 part_v[:, r, b.graphs, :]).then_inc(s_part_in[b.slot], 16)

            blocks(sp, load_parts)
            sp.wait_ge(s_out, 16 * BLOCKS)

        def steps(eng, step, depth):
            peeled = (depth + 3) // 2 * 2
            def lagged(i):
                return [Group(0, i - lag) if 0 <= i - lag < GROUPS else None for lag in range(depth + 1)]
            for i in range(peeled):
                step(i, lagged(i))
            with eng.Fori(peeled // 2, GROUPS // 2) as k:
                for u in range(2):
                    step(None, [Group(k, u - lag) for lag in range(depth + 1)])
            for i in range(GROUPS, GROUPS + depth):
                step(i, lagged(i))

        def tile_steps(eng, step):
            def tiles(t):
                return [Tile(0, t - n) if 0 <= t - n < TILES else None for n in range(4)]
            for t in range(8):
                step(*tiles(t))
            with eng.Fori(1, TILES // 8) as k:
                for v in range(8):
                    step(*(Tile(k * 2, v - n) for n in range(4)))
            for t in range(TILES // 8 * 8, TILES + 3):
                step(*tiles(t))

        @block.gpsimd
        def _(pool):
            wait = waiter(pool)
            pool.memset(bias_f[:, :], 0.0)
            pool.memset(b2_f[:, :], 0.0).then_inc(s_rows_zero, 1)
            pool.memset(ident32[:, :], 0.0)
            pool.memset(ident16[:, :], 0.0)
            pool.memset(earlier[:, :], 1.0)
            pool.memset(ones16[:, :], 1.0)
            pool.memset(minus_mean[:, :], -WS / D)
            pool.memset(plus_mean[:, :], WS / D)
            pool.memset(bias_gain[:, :], 1.0 / BS)
            pool.memset(out_gain[:, :], HS * WS / BS)
            pool.memset(half_power[:, :], -0.5)
            pool.memset(seen[:, :], 0.0)
            pool.iota(expert_no[:, :], pattern=[[1, EXPERTS]], base=0, channel_multiplier=0,
                      allow_small_or_imprecise_dtypes=True)
            pool.iota(region_start[:, :, :], pattern=[[0, J], [REGION, EXPERTS]], base=0, channel_multiplier=0,
                      allow_small_or_imprecise_dtypes=True)
            pool.iota(tile_no[:, :], pattern=[[1, TILES]], base=0, channel_multiplier=0,
                      allow_small_or_imprecise_dtypes=True)
            for n in range(2):
                last = pool.iota(row32[:, n, :, :, D + 1], pattern=[[1, J], [TOKENS, RANKS]], base=J * n,
                                 channel_multiplier=GRAPHS)
            last.then_inc(s_zero, 1)
            pool.wait_ge(s_zero, 1)
            pool.affine_select(out=ident32[:, :], in_=ident32[:, :], compare_op=ALU.not_equal, fill=1.0, base=0,
                               pattern=[[-1, 128]], channel_multiplier=1)
            pool.affine_select(out=ident16[:, :], in_=ident16[:, :], compare_op=ALU.not_equal, fill=1.0, base=0,
                               pattern=[[-1, 128]], channel_multiplier=1)
            pool.affine_select(out=earlier[:, :], in_=earlier[:, :], compare_op=ALU.is_gt, fill=0.0, base=0,
                               pattern=[[1, 128]], channel_multiplier=-1).then_inc(s_cpool, 1)

            def make_padding():
                pool.memset(pad[:, :, :, :], 0.0).then_inc(s_zero, 1)
                pool.wait_ge(s_zero, 2)
                pool.iota(pad32[:, :, :, D + 1], pattern=[[TILE, PADS], [1, 2]], base=RANKS * TOKENS,
                          channel_multiplier=2).then_inc(s_pad, 1)

            def rstd_of_x(g):
                if not g:
                    return
                wait(s_veps1, g.done)
                wait(s_xn, g.number)
                pool.tensor_tensor(rstd1[:, :], veps1[:, :], half_power[:, :], ALU.pow).then_inc(s_rstd1, 1)

            def rstd_of_x2(g):
                if not g:
                    return
                wait(s_veps2, g.done)
                wait(s_xs, g.number)
                pool.tensor_tensor(rstd2[:, :], veps2[:, :], half_power[:, :], ALU.pow).then_inc(s_rstd2, 1)

            def destinations(g):
                if not g or (isinstance(g.number, int) and g.number < 2):
                    return
                wait_apart(pool, (s_scattered[g.slot], g.half * (16 * J * RANKS)))
                dest = row32[:, g.slot, :, :, D + 1]
                pool.tensor_scalar(dest, dest, 2 * J, None, ALU.add).then_inc(s_dest, 1)

            def scatter(g, j):
                if not g:
                    return
                if j == 0:
                    wait_apart(pool, (s_slots, g.done), (s_pack, g.done), (s_w_ranks, g.done), (s_dest, g.number - 1))
                for r in range(RANKS):
                    pool.indirect_dma_start(
                        routed, bass.IndirectOffsetOnAxis(ap=slots[:, g.slot, r, j:j + 1], axis=0),
                        row[:, g.slot, j, r, :], None).then_inc(s_scattered[g.slot], 16)

            def step(i, g):
                rstd_of_x2(g[2])
                scatter(g[4], 2)
                scatter(g[4], 3)
                if i == 3:
                    make_padding()
                rstd_of_x(g[0])
                scatter(g[3], 0)
                scatter(g[3], 1)
                destinations(g[2])

            steps(pool, step, 4)

            def tile_step(tx, t0, t1, t2):
                if t2:
                    wait_apart(pool, (t_y, t2.done))
                    for a in range(2):
                        pool.indirect_dma_start(
                            parts, bass.IndirectOffsetOnAxis(ap=meta32[:, t2.slot4, a, 1:2], axis=0),
                            y[:, t2.slot, a, :], None).then_inc(s_y_out[t2.slot], 16)
                if t0:
                    wait(s_rows_in[t0.slot4], (t0.quarter + 1) * 16)
                    wait(s_y_out[t0.slot], (t0.half - 1) * 32)
                    wait_apart(pool, (t_y, t0.number - 3))
                    pool.tensor_copy(meta32[:, t0.slot4, :, :], rows32[:, t0.slot4, :, D:D + 2]).then_inc(t_meta, 1)

            tile_steps(pool, tile_step)

            def add_parts(b):
                wait(s_part_in[b.slot], (b.uses + 1) * 32)
                pool.tensor_tensor(part_t[:, b.slot, 0, :, :], part_t[:, b.slot, 0, :, :], part_t[:, b.slot, 1, :, :],
                                   ALU.add).then_inc(s_part_sum, 1)

            blocks(pool, add_parts)

        @block.scalar
        def _(act):
            wait = waiter(act)

            def high_graph_bias():
                act.wait_ge(s_gb_scaled, 1)
                act.activation(bias_rows[:, :], bias_f[:, :], ACT.Copy).then_inc(s_gb_hi, 1)

            def high_router():
                act.wait_ge(s_wrsum, 1)
                act.activation(wr16[:, 0, :], wr_shift[:, :], ACT.Copy).then_inc(s_wr_hi, 1)

            def high_b2():
                act.wait_ge(s_b2_scaled, 1)
                act.activation(b2_16[:, :], b2_f[:, :], ACT.Copy).then_inc(s_b2_hi, 1)

            def w2_high(n):
                at = SPLIT_ORDER[n] * WSPAN + 2 * F
                act.wait_ge(s_w_in[n % 2], 48 * (n // 2 + 1))
                act.activation(w16[:, at:at + F], w_in[:, n % 2, 1, :], ACT.Copy, scale=WS).then_inc(s_w2hi, 1)

            def w1_high(n):
                at = SPLIT_ORDER[n] * WSPAN
                act.wait_ge(s_w1sum, n + 1)
                act.activation(w16[:, at:at + F], w_shift[:, :], ACT.Copy).then_inc(s_w1hi, 1)

            def gelu(g, u):
                if not g:
                    return
                m = g.number * C + u + 1
                wait(s_up, m)
                wait(s_hlo, m - 2)
                act.activation(h[:, u % 2, :], banks[:, 4 + u % 2, :], ACT.Gelu,
                               scale=1.0 / (XS * WS)).then_inc(s_gelu, 1)

            def high(g, u):
                if not g:
                    return
                wait(s_gelu, g.number * C + u + 1)
                if u == 0:
                    wait(s_down, g.number - 1)
                act.activation(h16[:, g.slot, 0, u, :], h[:, u % 2, :], ACT.Copy, scale=HS).then_inc(s_hhi, 1)

            def x_high(g):
                if not g:
                    return
                wait(s_xs, g.done)
                wait(s_x_turned, g.number)
                wait(s_pack, g.number)
                act.activation(x16[:, :, 0:D], xs[:, :, :], ACT.Copy, bias=XS).then_inc(s_hi, 1)

            def normalize1(g):
                if not g:
                    return
                wait(s_xn_bias, g.done)
                wait(s_z, g.number)
                for j in range(J):
                    last = act.activation(xn[:, j, :], x_t[:, g.slot, j, :], ACT.Identity, bias=xn_bias[:, j:j + 1],
                                          scale=rstd1[:, j:j + 1])
                last.then_inc(s_xn, 1)

            def copy_zT(g):
                if not g:
                    return
                wait(s_z, g.done)
                wait(s_g, g.number)
                act.activation(zT[:, :, :], bank_z, ACT.Copy).then_inc(s_zT, 1)

            def copy_adjT(g):
                if not g:
                    return
                wait(s_adj_turned, g.done)
                wait(s_z, g.number)
                act.activation(adjT[:, :, :], bank_z, ACT.Copy).then_inc(s_adjT, 1)

            def copy_xT(g):
                if not g:
                    return
                wait(s_x_turned, g.done)
                wait(s_up, (g.number - 1) * C)
                wait(s_logits, g.number - 1)
                act.activation(xT[:, g.slot, :, :], bank_x, ACT.Copy).then_inc(s_xT, 1)

            def gap_tanh(g):
                if not g:
                    return
                wait(s_gap, g.done)
                wait(s_w_ranks, g.number)
                act.activation(half_tanh[:, :], gap[:, :], ACT.Tanh, scale=0.5 / (XS * WS)).then_inc(s_tanh, 1)

            def pack_rows(g):
                if not g:
                    return
                wait(s_lo, g.done)
                wait(s_scattered[g.slot], g.half * (16 * J * RANKS))
                act.activation(row[:, g.slot, :, :, 0:D],
                               x16[:, :, :].bitcast(F32).rearrange("p j (r d) -> p j r d", r=1).to_broadcast(
                                   [128, J, RANKS, D]), ACT.Copy).then_inc(s_pack, 1)

            def step(i, g):
                if i == 5:
                    w1_high(6)
                high(g[4], 3)
                if i == 3:
                    w2_high(5)
                if i == 5:
                    w2_high(7)
                gelu(g[3], 0)
                if i == 3:
                    w1_high(4)
                high(g[3], 0)
                if i == 2:
                    w2_high(3)
                copy_xT(g[2])
                if i == 0:
                    w2_high(0)
                    w2_high(1)
                copy_adjT(g[0])
                if i == 0:
                    w1_high(0)
                    high_graph_bias()
                if i == 1:
                    w1_high(1)
                if i == 2:
                    w1_high(3)
                normalize1(g[0])
                if i == 3:
                    high_b2()
                if i == 5:
                    w1_high(7)
                gelu(g[3], 1)
                pack_rows(g[2])
                high(g[3], 1)
                if i == 5:
                    w2_high(8)
                gelu(g[3], 2)
                if i == 3:
                    w2_high(6)
                high(g[3], 2)
                if i == 1:
                    high_router()
                    w2_high(2)
                if i == 2:
                    w2_high(4)
                copy_zT(g[0])
                if i == 3:
                    w1_high(5)
                gap_tanh(g[2])
                if i == 1:
                    w1_high(2)
                if i == 5:
                    w1_high(8)
                x_high(g[1])
                gelu(g[3], 3)

            steps(act, step, 4)

            act.wait_ge(s_table, 1)

            def tile_step(tx, t0, t1, t2):
                def unit(u):
                    n = t0.number * 2 + u + 1
                    wait(t_up, n)
                    wait(t_hlo, n - 2)
                    act.activation(h[:, u, :], banks[:, 4 + u, :], ACT.Gelu, scale=1.0 / (XS * WS)).then_inc(t_gelu, 1)
                    wait(t_gelu, n)
                    wait(t_down, t0.number - 1)
                    act.activation(h16[:, t0.slot, 0, u, :], h[:, u, :], ACT.Copy, scale=HS).then_inc(t_hhi, 1)

                if t0:
                    unit(0)
                if t2:
                    wait(t_y_b, t2.done)
                    wait(s_y_out[t2.slot], t2.half * 32)
                    wait(t_meta, t2.done)
                    for a in range(2):
                        last = act.activation(y[:, t2.slot, a, :], y_b[:, t2.slot, a, :], ACT.Copy,
                                              scale=meta[:, t2.slot4, a, 0:1])
                    last.then_inc(t_y, 1)
                if t0:
                    unit(1)

            tile_steps(act, tile_step)

            out_v = out.rearrange("b n d -> n b d")

            def store(b):
                wait(s_sum, b.done)
                act.dma_start(out_v[:, b.graphs, :], x2[:, b.graphs, :]).then_inc(s_out, 16)

            blocks(act, store)

        @block.tensor
        def _(pe):
            wait = waiter(pe)
            pe.wait_ge(s_cpool, 1)

            def shift_router():
                pe.wait_ge(s_const_in, 64)
                pe.matmul(banks[:, 2, 0:EXPERTS], minus_mean[:, :], wr_in[:, :], start=True, stop=True).then_inc(s_wr_shift, 1)

            def shift_weights(n):
                pe.wait_ge(s_w_in[n % 2], 48 * (n // 2 + 1))
                wait(s_w1sum, n)
                bank = banks[:, 7, :]
                pe.matmul(bank, minus_mean[:, :], w_in[:, n % 2, 0, :], start=True, stop=False)
                pe.matmul(bank, plus_mean[:, :], b_in[:, n % 2, :], start=False, stop=True).then_inc(s_shift, 1)

            def first(g):
                return isinstance(g.number, int) and g.number == 0

            def count_rows():
                pe.wait_ge(s_seen, GROUPS)
                pe.wait_ge(s_place, GROUPS)
                pe.wait_ge(s_top_at, GROUPS)
                pe.matmul(bank_l[:, 0:EXPERTS], ones16[:, :], seen[:, :], start=True, stop=True).then_inc(s_counts, 1)

            def up(g, u):
                if not g:
                    return
                wait(s_gelu, g.number * C + u - 1)
                if u == 0:
                    wait(s_xT, g.done)
                if u == 0 and first(g):
                    pe.wait_ge(s_w1lo, 1)
                for m, (a, b) in enumerate(PARTS):
                    mm = pe.matmul(banks[:, 4 + u % 2, :], w16_at(SHARED * WSPAN, 0, a, u), xT[:, g.slot, b, :],
                                   start=m == 0, stop=m == 2)
                mm.then_inc(s_up, 1)

            def down(g, u):
                if not g:
                    return
                if u == 0:
                    if first(g):
                        pe.wait_ge(s_w2lo, 1)
                        pe.wait_ge(s_b2_lo, 1)
                    wait(s_y, g.number)
                    pe.matmul(bank_y(0), out_gain[:, :],
                              b2_16[:, :].rearrange("p (a d) -> p a d", a=1).to_broadcast([64, J, D]), start=True, stop=False,
                              skip_group_check=True)
                wait(s_hlo, g.number * C + u + 1)
                for j in range(J):
                    for a, b in PARTS:
                        mm = pe.matmul(bank_y(0)[:, j * D:(j + 1) * D], h16[:, g.slot, b, u, j * NODES:(j + 1) * NODES],
                                       w16_at(SHARED * WSPAN, 1, a, u), start=False, stop=u == C - 1,
                                       skip_group_check=True)
                if u == C - 1:
                    mm.then_inc(s_down, 1)

            def turn_adj(g):
                if not g:
                    return
                wait(s_adj_in[g.slot], (g.half + 1) * 16)
                wait(s_zT, g.number)
                for j in range(J):
                    mm = pe.transpose(bank_z[:, j, :], adj_t[:, g.slot, j, :], ident32[:, :])
                mm.then_inc(s_adj_turned, 1)

            def aggregate(g):
                if not g:
                    return
                wait(s_adjT, g.done)
                wait(s_xn, g.done)
                for j in range(J):
                    mm = pe.matmul(bank_z[:, j, :], xn[:, j, :], adjT[:, j, :], start=True, stop=True)
                mm.then_inc(s_z, 1)

            def graph_product(g):
                if not g:
                    return
                wait(s_zT, g.done)
                wait(s_x2, g.number)
                if first(g):
                    pe.wait_ge(s_const_in, 64)
                    pe.wait_ge(s_gb_lo, 1)
                pe.matmul(bank_g, bias_gain[:, :],
                          bias_rows[:, :].rearrange("p (a d) -> p a d", a=1).to_broadcast([64, J, D]), start=True, stop=False,
                          skip_group_check=True)
                for j in range(J):
                    mm = pe.matmul(bank_g[:, j, :], zT[:, j, :], wg[:, :], start=False, stop=True,
                                   skip_group_check=True)
                mm.then_inc(s_g, 1)

            def turn_x_group(g):
                if not g:
                    return
                wait(s_hi, g.done)
                wait(s_lo, g.done)
                wait(s_xT, g.number)
                if first(g):
                    pe.wait_ge(s_wrsum, 1)
                for a in range(2):
                    for j in range(J):
                        mm = pe.transpose(bank_x[:, a, j * D:(j + 1) * D], x16[:, j, a * D:(a + 1) * D],
                                          ident16[:, :])
                mm.then_inc(s_x_turned, 1)

            def router_logits(g):
                if not g:
                    return
                wait(s_xT, g.done)
                wait(s_top_at, g.number)
                wait(s_place, g.number)
                if first(g):
                    pe.wait_ge(s_wr_lo, 1)
                for j in range(J):
                    for m, (a, b) in enumerate(PARTS):
                        mm = pe.matmul(logits[:, j, :], xT[:, g.slot, b, j * NODES:(j + 1) * NODES],
                                       wr16[:, a, :], start=m == 0, stop=m == 2)
                mm.then_inc(s_logits, 1)

            def count_before(g):
                if not g:
                    return
                wait(s_both, g.done)
                wait(s_seen, g.number)
                wait(s_top_at, g.done)
                pe.matmul(before, earlier[:, :], both[:, :, :], start=True, stop=False, skip_group_check=True)
                pe.matmul(before, ones16[:, :],
                          seen[:, :].rearrange("p (a e) -> p a e", a=1).to_broadcast([128, J, EXPERTS]),
                          start=False, stop=False, skip_group_check=True)
                for j in range(J - 1):
                    mm = pe.matmul(before[:, j + 1:J, :], ones16[:, :],
                                   both[:, j:j + 1, :].to_broadcast([128, J - 1 - j, EXPERTS]),
                                   start=False, stop=j == J - 2, skip_group_check=True)
                mm.then_inc(s_before, 1)

            def step(i, g):
                up(g[4], 3)
                up(g[3], 0)
                if i == 2:
                    shift_weights(3)
                graph_product(g[1])
                if i == 0:
                    shift_weights(0)
                turn_adj(g[0])
                if i == 5:
                    shift_weights(7)
                turn_x_group(g[2])
                down(g[4], 0)
                down(g[4], 1)
                if i == 3:
                    shift_weights(5)
                router_logits(g[2])
                up(g[3], 1)
                if i == 18:
                    count_rows()
                up(g[3], 2)
                down(g[4], 2)
                if i == 0:
                    shift_weights(1)
                if i == 1:
                    shift_router()
                    shift_weights(2)
                if i == 2:
                    shift_weights(4)
                if i == 5:
                    shift_weights(8)
                aggregate(g[0])
                if i == 3:
                    shift_weights(6)
                count_before(g[2])
                down(g[4], 3)

            steps(pe, step, 4)

            pe.wait_ge(s_table, 1)
            pe.wait_ge(s_xT, GROUPS)
            pe.wait_ge(s_y, GROUPS)
            pe.wait_ge(s_w1lo, EXPERTS + 1)
            pe.wait_ge(s_w1hi, EXPERTS + 1)
            pe.wait_ge(s_w2lo, EXPERTS + 1)
            pe.wait_ge(s_w2hi, EXPERTS + 1)

            def turn_x(t):
                wait(s_rows_in[t.slot4], (t.quarter + 1) * 16)
                wait(t_xT, t.number)
                for a in range(2):
                    for b in range(2):
                        mm = pe.transpose(bank_x[:, b, a * 128:(a + 1) * 128],
                                          rows16[:, t.slot4, a, b * D:(b + 1) * D], ident16[:, :])
                mm.then_inc(t_x_turned, 1)

            def tile_step(tx, t0, t1, t2):
                if tx and not t0:
                    turn_x(tx)
                if t0:
                    at = pe.value_load(tile_w[0:1, bass.ds(t0.number, 1)], min_val=0, max_val=(EXPERTS - 1) * WSPAN)
                    wait(t_xT, t0.done)
                    for u in range(2):
                        wait(t_gelu, t0.number * 2 + u - 1)
                        for v in range(2):
                            for m, (a, b) in enumerate(PARTS):
                                mm = pe.matmul(banks[:, 4 + u, v * TILE:(v + 1) * TILE], w16_at(at, 0, a, 2 * u + v),
                                               xT[:, t0.slot, b, 0:TILE], start=m == 0, stop=m == 2)
                        mm.then_inc(t_up, 1)
                        if tx and u == 0:
                            turn_x(tx)
                if t1:
                    bank = bank_y(t1.slot)[:, 0:2 * D]
                    wait(s_w2_in[t1.slot4], (t1.quarter + 1) * 16)
                    wait(t_y_b, t1.number - 1)
                    for p in range(2):
                        for c in range(C):
                            if p == 0 and c % 2 == 0:
                                wait(t_hlo, t1.number * 2 + c // 2 + 1)
                            for m, (a, b) in enumerate(PARTS):
                                at = c % 2 * TILE + p * 128
                                mm = pe.matmul(bank[:, p * D:(p + 1) * D], h16[:, t1.slot, b, c // 2, at:at + 128],
                                               w2_t[:, t1.slot4, a * F + c * D:a * F + (c + 1) * D],
                                               start=c == 0 and m == 0, stop=c == C - 1 and m == 2)
                    mm.then_inc(t_down, 1)

            tile_steps(pe, tile_step)

        @block.vector
        def _(dve):
            wait = waiter(dve)

            def scale_graph_bias():
                dve.wait_ge(s_const_in, 64)
                dve.tensor_scalar(bias_f[:, :], bias_f[:, :], BS, None, ALU.mult).then_inc(s_gb_scaled, 1)

            def low_graph_bias():
                dve.wait_ge(s_gb_hi, 1)
                dve.tensor_tensor(bias_rows[32:33, :], bias_f[32:33, :], bias_rows[32:33, :],
                                  ALU.subtract).then_inc(s_gb_lo, 1)

            def sum_router():
                dve.wait_ge(s_wr_shift, 1)
                dve.scalar_tensor_tensor(out=wr_shift[:, :], in0=wr_in[:, :], scalar=WS, in1=banks[:, 2, 0:EXPERTS],
                                         op0=ALU.mult, op1=ALU.add).then_inc(s_wrsum, 1)

            def low_router():
                dve.wait_ge(s_wr_hi, 1)
                dve.tensor_tensor(wr16[:, 1, :], wr_shift[:, :], wr16[:, 0, :], ALU.subtract).then_inc(s_wr_lo, 1)

            def scale_b2():
                dve.wait_ge(s_b2_in, 32)
                dve.tensor_scalar(b2_f[:, :], b2_f[:, :], BS, None, ALU.mult).then_inc(s_b2_scaled, 1)

            def low_b2():
                dve.wait_ge(s_b2_hi, 1)
                dve.tensor_tensor(b2_16[32:33, :], b2_f[32:33, :], b2_16[32:33, :], ALU.subtract).then_inc(s_b2_lo, 1)

            def sum_weights(n):
                dve.wait_ge(s_shift, n + 1)
                wait(s_w1lo, n)
                wait(s_w1hi, n)
                dve.scalar_tensor_tensor(out=w_shift[:, :], in0=w_in[:, n % 2, 0, :], scalar=WS,
                                         in1=banks[:, 7, :], op0=ALU.mult, op1=ALU.add).then_inc(s_w1sum, 1)

            def w2_low(n):
                at = SPLIT_ORDER[n] * WSPAN
                dve.wait_ge(s_w2hi, n + 1)
                dve.scalar_tensor_tensor(out=w16[:, at + 3 * F:at + 4 * F], in0=w_in[:, n % 2, 1, :], scalar=WS,
                                         in1=w16[:, at + 2 * F:at + 3 * F], op0=ALU.mult,
                                         op1=ALU.subtract).then_inc(s_w2lo, 1)

            def w1_low(n):
                at = SPLIT_ORDER[n] * WSPAN
                dve.wait_ge(s_w1hi, n + 1)
                dve.tensor_tensor(w16[:, at + F:at + 2 * F], w_shift[:, :], w16[:, at:at + F],
                                  ALU.subtract).then_inc(s_w1lo, 1)

            def make_table():
                links = [0]

                def link(ins):
                    links[0] += 1
                    ins.then_inc(s_chain, 1)
                    dve.wait_ge(s_chain, links[0])

                dve.wait_ge(s_counts, 1)
                link(dve.tensor_copy(counts[:, :], bank_l[0:1, 0:EXPERTS]))
                dve.tensor_tensor(pad_at[:, :], counts[:, :], region_start[0:1, 0, :], ALU.add).then_inc(s_pad_at, 1)
                link(dve.tensor_scalar(tiles_i[:, 0, :], counts[:, :], TILE - 1.0, None, ALU.add))
                link(dve.tensor_scalar(tiles_i[:, 1, :], tiles_i[:, 0, :], TILE.bit_length() - 1, None,
                                       ALU.logical_shift_right))
                link(dve.tensor_copy(tiles_end[:, 0, :], tiles_i[:, 1, :]))
                dve.tensor_scalar(region_step[:, :], tiles_end[:, 0, :], -float(TILE), float(REGION), ALU.mult, ALU.add)
                for n, s in enumerate((1, 2, 4)):
                    dve.tensor_copy(tiles_end[:, n + 1, 0:s], tiles_end[:, n, 0:s])
                    link(dve.tensor_tensor(tiles_end[:, n + 1, s:], tiles_end[:, n, s:],
                                           tiles_end[:, n, 0:EXPERTS - s], ALU.add))
                every = [1, TILES, EXPERTS]
                over_e = lambda v: v.rearrange("p (a e) -> p a e", a=1).to_broadcast(every)
                over_t = lambda v: v.rearrange("p (t a) -> p t a", a=1).to_broadcast(every)
                link(dve.tensor_tensor(past[:, :, :], over_e(tiles_end[:, 3, :]), over_t(tile_no[:, :]), ALU.is_le))
                link(dve.tensor_tensor(past_steps[:, :, :], past[:, :, :], over_e(region_step[:, :]), ALU.mult))
                link(dve.tensor_reduce(row_steps[:, :], past_steps[:, :, :], AX.X, ALU.add))
                dve.scalar_tensor_tensor(out=tile_row[:, :], in0=tile_no[:, :], scalar=float(TILE),
                                         in1=row_steps[:, :], op0=ALU.mult, op1=ALU.add)
                link(dve.tensor_reduce(tile_e[:, :], past[:, :, :], AX.X, ALU.add))
                dve.tensor_scalar(tile_word[:, :], tile_e[:, :], EXPERTS - 1.0, WSPAN / 2.0, ALU.min, ALU.mult)
                dve.tensor_scalar(tile_w[:, :], tile_e[:, :], EXPERTS - 1.0, float(WSPAN), ALU.min,
                                  ALU.mult).then_inc(s_table, 1)

            def x2_of(g):
                return x2[:, bass.ds(g.number * J, J), :]

            def x2_graph(g, j):
                return x2[:, bass.ds(g.number * J + j, 1), :].rearrange("p a d -> p (a d)")

            def stats_of_x(g):
                if not g:
                    return
                wait_apart(dve, (s_x_in[g.slot], (g.half + 1) * 16))
                for j in range(J):
                    last = dve.bn_stats(stats1[:, j, :], x_t[:, g.slot, j, :])
                last.then_inc(s_stats1, 1)

            def moments_of_x(g):
                if not g:
                    return
                wait_apart(dve, (s_stats1, g.done))
                for j in range(J):
                    last = dve.bn_aggr(mom1[:, j, :], stats1[:, j, :])
                last.then_inc(s_mom1, 1)

            def variance_of_x(g):
                if not g:
                    return
                wait(s_mom1, g.done)
                wait(s_rstd1, g.number)
                dve.tensor_scalar(veps1[:, :], mom1[:, :, 1], EPS, None, ALU.add).then_inc(s_veps1, 1)

            def normalize_bias(g):
                if not g:
                    return
                wait(s_rstd1, g.done)
                wait(s_xn, g.number)
                dve.scalar_tensor_tensor(out=xn_bias[:, :], in0=mom1[:, :, 0], scalar=-1.0, in1=rstd1[:, :],
                                         op0=ALU.mult, op1=ALU.mult).then_inc(s_xn_bias, 1)

            def add_graph(g):
                if not g:
                    return
                wait(s_g, g.done)
                dve.tensor_tensor(x2_of(g), bank_g, x_t[:, g.slot, :, :], ALU.add).then_inc(s_x2, 1)

            def stats_of_x2(g):
                if not g:
                    return
                wait_apart(dve, (s_x2, g.done))
                for j in range(J):
                    last = dve.bn_stats(stats2[:, j, :], x2_graph(g, j))
                last.then_inc(s_stats2, 1)

            def moments_of_x2(g):
                if not g:
                    return
                wait_apart(dve, (s_stats2, g.done))
                for j in range(J):
                    last = dve.bn_aggr(mom2[:, j, :], stats2[:, j, :])
                last.then_inc(s_mom2, 1)

            def variance_of_x2(g):
                if not g:
                    return
                wait(s_mom2, g.done)
                wait(s_rstd2, g.number)
                dve.tensor_scalar(veps2[:, :], mom2[:, :, 1], EPS, XS ** -2, ALU.add, ALU.mult).then_inc(s_veps2, 1)

            def normalize2(g):
                if not g:
                    return
                wait(s_rstd2, g.done)
                wait(s_hi, g.number)
                wait(s_lo, g.number)
                for j in range(J):
                    last = dve.tensor_scalar(xs[:, j, :], x2_graph(g, j), mom2[:, j, 0:1], rstd2[:, j:j + 1],
                                             ALU.subtract, ALU.mult)
                last.then_inc(s_xs, 1)

            def x_low(g):
                if not g:
                    return
                wait(s_hi, g.done)
                dve.scalar_tensor_tensor(out=x16[:, :, D:2 * D], in0=xs[:, :, :], scalar=XS,
                                         in1=x16[:, :, 0:D], op0=ALU.add, op1=ALU.subtract).then_inc(s_lo, 1)

            def top_values(g):
                if not g:
                    return
                wait_apart(dve, (s_logits, g.done))
                for j in range(J):
                    last = dve.max(out=top[:, j, :], in_=logits[:, j, :])
                last.then_inc(s_top, 1)

            def top_indices(g):
                if not g:
                    return
                wait_apart(dve, (s_top, g.done))
                for j in range(J):
                    last = dve.max_index(top_at[:, j, :], top[:, j, :], logits[:, j, :])
                last.then_inc(s_top_at, 1)

            def logit_gap(g):
                if not g:
                    return
                wait(s_top, g.done)
                wait(s_tanh, g.number)
                dve.tensor_tensor(gap[:, :], top[:, :, 0], top[:, :, 1], ALU.subtract).then_inc(s_gap, 1)

            def router_weights(g):
                if not g:
                    return
                wait(s_tanh, g.done)
                wait(s_scattered[g.slot], g.half * (16 * J * RANKS))
                for r in range(RANKS):
                    last = dve.tensor_scalar(row[:, g.slot, :, r, D], half_tanh[:, :], 0.5 - r, 0.5,
                                             ALU.mult, ALU.add)
                last.then_inc(s_w_ranks, 1)

            def pick_numbers(g):
                if not g:
                    return
                wait(s_top_at, g.done)
                dve.tensor_copy(pick_no[:, :, :], top_at[:, :, 0:RANKS].rearrange("p j r -> p r j")).then_inc(
                    s_pick_no, 1)

            def one_hots(g):
                if not g:
                    return
                wait(s_pick_no, g.done)
                for r in range(RANKS):
                    last = dve.tensor_tensor(
                        picks[:, r, :, :],
                        expert_no[:, :].rearrange("p (a e) -> p a e", a=1).to_broadcast([128, J, EXPERTS]),
                        pick_no[:, r, :].rearrange("p (j a) -> p j a", a=1).to_broadcast([128, J, EXPERTS]),
                        ALU.is_equal)
                last.then_inc(s_picks, 1)

            def both_picks(g):
                if not g:
                    return
                wait(s_picks, g.done)
                wait(s_before, g.number)
                wait(s_seen_now, g.number)
                dve.tensor_tensor(both[:, :, :], picks[:, 0, :, :], picks[:, 1, :, :], ALU.add).then_inc(s_both, 1)

            def count_picks(g):
                if not g:
                    return
                wait(s_both, g.done)
                dve.tensor_reduce(seen_now[:, :], both[:, :, :].rearrange("p j e -> p e j"), AX.X,
                                  ALU.add).then_inc(s_seen_now, 1)

            def add_to_seen(g):
                if not g:
                    return
                wait(s_seen_now, g.done)
                wait(s_before, g.done)
                dve.tensor_tensor(seen[:, :], seen[:, :], seen_now[:, :], ALU.add).then_inc(s_seen, 1)

            def places(g):
                if not g:
                    return
                wait(s_before, g.done)
                dve.tensor_tensor(place[:, :, :], before, region_start[:, :, :], ALU.add).then_inc(s_place, 1)

            def places_of_picks(g):
                if not g:
                    return
                wait(s_place, g.done)
                for r in range(RANKS):
                    last = dve.tensor_tensor(place_of[:, r, :, :], picks[:, r, :, :], place[:, :, :], ALU.mult)
                last.then_inc(s_place_of, 1)

            def row_numbers(g):
                if not g:
                    return
                wait(s_place_of, g.done)
                wait(s_scattered[g.slot], g.half * (16 * J * RANKS))
                with nc.allow_low_precision(reason="one row number of those summed is not zero"):
                    dve.tensor_reduce(slots[:, g.slot, :, :], place_of[:, :, :, :], AX.X,
                                      ALU.add).then_inc(s_slots, 1)

            def low(g, u):
                if not g:
                    return
                wait(s_hhi, g.number * C + u + 1)
                dve.scalar_tensor_tensor(out=h16[:, g.slot, 1, u, :], in0=h[:, u % 2, :], scalar=HS,
                                         in1=h16[:, g.slot, 0, u, :], op0=ALU.mult,
                                         op1=ALU.subtract).then_inc(s_hlo, 1)

            def add_shared(g):
                if not g:
                    return
                wait(s_down, g.done)
                dve.scalar_tensor_tensor(out=x2_of(g), in0=bank_y(0).rearrange("p (j d) -> p j d", j=J),
                                         scalar=1.0 / (HS * WS), in1=x2_of(g), op0=ALU.mult,
                                         op1=ALU.add).then_inc(s_y, 1)

            def step(i, g):
                if i == 4:
                    sum_weights(5)
                top_values(g[3])
                if i == 2:
                    w1_low(1)
                if i == 6:
                    sum_weights(7)
                moments_of_x2(g[2])
                top_indices(g[3])
                if i == 2:
                    scale_b2()
                    low_router()
                if i == 3:
                    w2_low(3)
                if i == 5:
                    w1_low(5)
                variance_of_x2(g[2])
                if i == 4:
                    w2_low(5)
                pick_numbers(g[3])
                if i == 4:
                    low_b2()
                if i == 6:
                    w1_low(7)
                logit_gap(g[3])
                if i == 3:
                    w1_low(3)
                if i == 5:
                    w2_low(6)
                one_hots(g[3])
                if i == 2:
                    sum_weights(2)
                    w2_low(2)
                stats_of_x(g[0])
                both_picks(g[3])
                normalize2(g[2])
                if i == 6:
                    sum_weights(8)
                if i == 7:
                    w1_low(8)
                low(g[4], 1)
                if i == 5:
                    sum_weights(6)
                moments_of_x(g[0])
                places(g[3])
                add_shared(g[5])
                router_weights(g[3])
                if i == 0:
                    w2_low(0)
                    scale_graph_bias()
                if i == 1:
                    w2_low(1)
                    low_graph_bias()
                if i == 2:
                    w1_low(2)
                if i == 5:
                    w1_low(6)
                variance_of_x(g[0])
                if i == 3:
                    sum_weights(4)
                places_of_picks(g[3])
                x_low(g[2])
                row_numbers(g[3])
                low(g[4], 2)
                if i == 1:
                    w1_low(0)
                    sum_weights(1)
                add_graph(g[1])
                if i == 3:
                    w2_low(4)
                if i == 6:
                    w2_low(8)
                count_picks(g[3])
                low(g[4], 3)
                if i == 0:
                    sum_weights(0)
                if i == 1:
                    sum_router()
                if i == 3:
                    w1_low(4)
                normalize_bias(g[0])
                if i == 2:
                    sum_weights(3)
                stats_of_x2(g[1])
                add_to_seen(g[3])
                if i == 5:
                    w2_low(7)
                if i == 18:
                    make_table()
                low(g[3], 0)

            steps(dve, step, 5)

            def tile_step(tx, t0, t1, t2):
                if tx:
                    wait(t_x_turned, tx.done)
                    wait(t_up, (tx.number - 1) * 2)
                    dve.tensor_copy(xT[:, tx.slot, :, 0:TILE], bank_x[:, :, 0:TILE]).then_inc(t_xT, 1)

                def low(u):
                    wait(t_hhi, t0.number * 2 + u + 1)
                    dve.scalar_tensor_tensor(out=h16[:, t0.slot, 1, u, :], in0=h[:, u, :], scalar=HS,
                                             in1=h16[:, t0.slot, 0, u, :], op0=ALU.mult,
                                             op1=ALU.subtract).then_inc(t_hlo, 1)

                if t0:
                    low(0)
                if t1:
                    wait(t_down, t1.done)
                    wait(t_y, t1.number - 1)
                    dve.scalar_tensor_tensor(out=y_b[:, t1.slot, :, :],
                                             in0=bank_y(t1.slot)[:, 0:2 * D].rearrange("p (a d) -> p a d", a=2),
                                             scalar=1.0 / (HS * WS),
                                             in1=w2_t32[:, t1.slot4:t1.slot4 + 1, F:F + D].to_broadcast([128, 2, D]),
                                             op0=ALU.mult, op1=ALU.add).then_inc(t_y_b, 1)
                if t0:
                    low(1)

            tile_steps(dve, tile_step)

            def add_routed(b):
                wait(s_part_sum, b.done)
                dve.tensor_tensor(x2[:, b.graphs, :], x2[:, b.graphs, :], part_t[:, b.slot, 0, :, :],
                                  ALU.add).then_inc(s_sum, 1)

            blocks(dve, add_routed)


_INS = ["x", "adj", "L0_gnn_weight", "L0_gnn_bias", "L0_ffn_Wr", "L0_ffn_W1s", "L0_ffn_b1s", "L0_ffn_W2s",
        "L0_ffn_b2s", "L0_ffn_W1p", "L0_ffn_b1p", "L0_ffn_W2p", "L0_ffn_b2p"]


def kernel(**inputs):
    import numpy as np
    import concourse.bacc as bacc
    from concourse import mybir as mb
    from concourse.bass_utils import run_bass_kernel_spmd

    nc = bacc.Bacc("TRN2", target_bir_lowering=False, num_devices=1)
    arrays, args = {}, []
    for name in _INS:
        a = np.ascontiguousarray(inputs[name])
        arrays[f"in_{name}"] = a
        args.append(nc.dram_tensor(f"in_{name}", a.shape, mb.dt.from_np(a.dtype), kind="ExternalInput").ap())
    args.append(nc.dram_tensor("out_0", (GRAPHS, NODES, D), mb.dt.from_np(np.dtype("float32")),
                               kind="ExternalOutput").ap())
    build(nc, *args)
    r = run_bass_kernel_spmd(nc, [arrays], core_ids=[0])
    return r.results[0]["out_0"]
```
